# Optimizing a Trainium2 kernel written in Bass

```python
import numpy as np
import jax
import jax.numpy as jnp

def _softmax(x, axis=-1):
    return jax.nn.softmax(x, axis=axis)

def _gelu(x):
    return jax.nn.gelu(x, approximate=True)

def _silu(x):
    return jax.nn.silu(x)

def _sigmoid(x):
    return jax.nn.sigmoid(x)

def _layernorm(x, axis=-1, eps=1e-05):
    m = jnp.mean(x, axis=axis, keepdims=True)
    v = jnp.var(x, axis=axis, keepdims=True)
    return (x - m) / jnp.sqrt(v + eps)

def _scatter_add(tgt, idx, src, axis=0):
    return tgt.at[idx].add(src)

def _segment_sum(src, seg, n):
    return jax.ops.segment_sum(src, seg, n)
kernel_name = 'mk_decoder_postln_d1_seqx_r8_a3af19'

def setup_inputs(seed: int=0):
    np.random.seed(seed)
    _w = jnp.asarray

    def _rec_inputs():
        import jax
        import jax.numpy as jnp
        _rk = jax.random.key(seed)
        x = -0.0002928 + 1 * jax.random.normal(jax.random.fold_in(_rk, 1), (128, 64, 128), jnp.float32)
        _lenS = 64 - jax.random.randint(jax.random.fold_in(_rk, 7), (128,), 0, max(1, 64 // 4) + 1, jnp.int32)
        _lenS2 = 64 - jax.random.randint(jax.random.fold_in(_rk, 8), (128,), 0, max(1, 64 // 4) + 1, jnp.int32)
        _ctx_1024P = jax.random.normal(jax.random.fold_in(_rk, 11), (128, 16, 128), jnp.float32)
        _ctx_1024c = jax.random.dirichlet(jax.random.fold_in(_rk, 511), 0.3 * jnp.ones((16,), jnp.float32), (128, 64))
        _ctx_1024t = jnp.einsum('bsk,bkd->bsd', _ctx_1024c, _ctx_1024P)
        _ctx_1024t = _ctx_1024t * jax.lax.rsqrt(jnp.mean(jnp.square(_ctx_1024t)) + 1e-12) * 0.953939
        ctx_1024 = -1.39393e-06 + 0.999914 * (_ctx_1024t + 0.3 * jax.random.normal(jax.random.fold_in(_rk, 611), (128, 64, 128), jnp.float32))
        return (x, ctx_1024)
    x, ctx_1024 = _rec_inputs()

    def _L0_attn_setup():
        import math
        import jax, jax.numpy as jnp
        import numpy as np
        N_HEAD = 16
        X_INT = -100.0
        Y_INT = 1.0
        POWER = 2
        DIVISOR = 1000.0

        def polymax(x):
            m = Y_INT / X_INT
            lin_cond = (x >= X_INT) & (x <= 0)
            x_lin = jnp.where(lin_cond, x, 0.0)
            lin = jnp.where(lin_cond, m * x_lin + Y_INT, 0.0)
            pos_cond = x > 0
            x_pos = jnp.where(pos_cond, x, 0.0)
            poly = jnp.where(pos_cond, x_pos ** POWER + Y_INT, 0.0)
            return (poly + lin) / DIVISOR
        key = jax.random.key(seed)
        k1, k2, k3 = jax.random.split(key, 3)
        B, T, C = (2, 256, 128)
        x = jax.random.normal(k1, (B, T, C), dtype=jnp.float32)
        W_attn = jax.random.normal(k2, (C, 3 * C), dtype=jnp.float32) * (1.0 / math.sqrt(C))
        W_proj = jax.random.normal(k3, (C, C), dtype=jnp.float32) * (1.0 / math.sqrt(C))
        return {'x': x, 'W_attn': W_attn, 'W_proj': W_proj}
    _L0_attn_all = _L0_attn_setup()
    _L0_attn_in = {k: v for k, v in _L0_attn_all.items() if k in ('W_attn', 'W_proj')}
    del _L0_attn_all

    def _L0_xattn_setup():
        import jax, jax.numpy as jnp
        import numpy as np
        import math
        D_MODEL = 128
        HEADS = 16
        DK = 64
        DV = 64
        key = jax.random.key(seed)
        ks = jax.random.split(key, 8)
        N, QL, KL = (2, 256, 256)
        s = 1.0 / math.sqrt(D_MODEL)
        return {'Q': jax.random.normal(ks[0], (N, QL, D_MODEL), jnp.float32), 'K': jax.random.normal(ks[1], (N, KL, D_MODEL), jnp.float32), 'V': jax.random.normal(ks[2], (N, KL, D_MODEL), jnp.float32), 'WQ': jax.random.normal(ks[3], (D_MODEL, HEADS * DK), jnp.float32) * s, 'WK': jax.random.normal(ks[4], (D_MODEL, HEADS * DK), jnp.float32) * s, 'WV': jax.random.normal(ks[5], (D_MODEL, HEADS * DV), jnp.float32) * s, 'WO': jax.random.normal(ks[6], (HEADS * DV, D_MODEL), jnp.float32) * (1.0 / math.sqrt(HEADS * DV)), 'bO': jnp.zeros((D_MODEL,), jnp.float32)}
    _L0_xattn_all = _L0_xattn_setup()
    _L0_xattn_in = {k: v for k, v in _L0_xattn_all.items() if k in ('WQ', 'WK', 'WV', 'WO', 'bO')}
    del _L0_xattn_all

    def _L0_ffn_setup():
        import jax, jax.numpy as jnp
        import numpy as np
        HIDDEN = 128
        NUM_EXPERTS = 16
        TOP_K = 6
        EPS = 1e-10
        key = jax.random.key(seed)
        k1, k2, k3, k4 = jax.random.split(key, 4)
        tokens = jax.random.normal(k1, (4, 256, HIDDEN), dtype=jnp.float32)
        bound = 1.0 / np.sqrt(HIDDEN)
        router_w = jax.random.uniform(k2, (NUM_EXPERTS, HIDDEN), jnp.float32, -bound, bound)
        router_b = jax.random.uniform(k3, (NUM_EXPERTS,), jnp.float32, -bound, bound)
        expert_w = jax.random.normal(k4, (NUM_EXPERTS, HIDDEN, HIDDEN), dtype=jnp.float32) / np.sqrt(HIDDEN)
        return {'tokens': tokens, 'router_w': router_w, 'router_b': router_b, 'expert_w': expert_w}
    _L0_ffn_all = _L0_ffn_setup()
    _L0_ffn_in = {k: v for k, v in _L0_ffn_all.items() if k in ('router_w', 'router_b', 'expert_w')}
    del _L0_ffn_all
    return {'x': x, 'ctx_1024': ctx_1024, 'L0_attn_W_attn': _L0_attn_in['W_attn'], 'L0_attn_W_proj': _L0_attn_in['W_proj'], 'L0_xattn_WQ': _L0_xattn_in['WQ'], 'L0_xattn_WK': _L0_xattn_in['WK'], 'L0_xattn_WV': _L0_xattn_in['WV'], 'L0_xattn_WO': _L0_xattn_in['WO'], 'L0_xattn_bO': _L0_xattn_in['bO'], 'L0_ffn_router_w': _L0_ffn_in['router_w'], 'L0_ffn_router_b': _L0_ffn_in['router_b'], 'L0_ffn_expert_w': _L0_ffn_in['expert_w']}

def reference(x, ctx_1024, L0_attn_W_attn, L0_attn_W_proj, L0_xattn_WQ, L0_xattn_WK, L0_xattn_WV, L0_xattn_WO, L0_xattn_bO, L0_ffn_router_w, L0_ffn_router_b, L0_ffn_expert_w):
    import jax
    import jax.numpy as jnp

    def _L0_attn_ref(x, W_attn, W_proj):
        import math
        import jax, jax.numpy as jnp
        import numpy as np
        N_HEAD = 16
        X_INT = -100.0
        Y_INT = 1.0
        POWER = 2
        DIVISOR = 1000.0

        def polymax(x):
            m = Y_INT / X_INT
            lin_cond = (x >= X_INT) & (x <= 0)
            x_lin = jnp.where(lin_cond, x, 0.0)
            lin = jnp.where(lin_cond, m * x_lin + Y_INT, 0.0)
            pos_cond = x > 0
            x_pos = jnp.where(pos_cond, x, 0.0)
            poly = jnp.where(pos_cond, x_pos ** POWER + Y_INT, 0.0)
            return (poly + lin) / DIVISOR
        B, T, C = x.shape
        H = N_HEAD
        hd = C // H
        qkv = x @ W_attn
        q, k, v = jnp.split(qkv, 3, axis=-1)
        q = q.reshape(B, T, H, hd).transpose(0, 2, 1, 3)
        k = k.reshape(B, T, H, hd).transpose(0, 2, 1, 3)
        v = v.reshape(B, T, H, hd).transpose(0, 2, 1, 3)
        att = jnp.einsum('bhid,bhjd->bhij', q, k) * (1.0 / math.sqrt(hd))
        causal = jnp.tril(jnp.ones((T, T), dtype=bool))
        att = jnp.where(causal[None, None], att, -jnp.inf)
        att = polymax(att)
        y = jnp.einsum('bhij,bhjd->bhid', att, v)
        y = y.transpose(0, 2, 1, 3).reshape(B, T, C)
        return y @ W_proj

    def _L0_xattn_ref(Q, K, V, WQ, WK, WV, WO, bO):
        import jax, jax.numpy as jnp
        import numpy as np
        import math
        D_MODEL = 128
        HEADS = 16
        DK = 64
        DV = 64
        N, ql, _ = Q.shape
        kl = K.shape[1]
        q = (Q @ WQ).reshape(N, ql, HEADS, DK)
        k = (K @ WK).reshape(N, kl, HEADS, DK)
        v = (V @ WV).reshape(N, kl, HEADS, DV)
        compat = jnp.einsum('nqhk,nlhk->nhql', q, k) / math.sqrt(DK)
        weights = jax.nn.softmax(compat, axis=3)
        attn = jnp.einsum('nhqk,nkhv->nqhv', weights, v).reshape(N, ql, HEADS * DV)
        return attn @ WO + bO

    def _L0_ffn_ref(tokens, router_w, router_b, expert_w):
        import jax, jax.numpy as jnp
        import numpy as np
        HIDDEN = 128
        NUM_EXPERTS = 16
        TOP_K = 6
        EPS = 1e-10
        B, S, H = tokens.shape
        E = expert_w.shape[0]
        T = B * S
        logits = jnp.einsum('bsh,eh->bse', tokens, router_w) + router_b
        probs = jax.nn.softmax(logits, axis=-1)
        top_p, top_i = jax.lax.top_k(probs, TOP_K)
        top_p = top_p / (jnp.sum(top_p, axis=-1, keepdims=True) + EPS)
        x = tokens.reshape(T, H)
        flat_i = top_i.reshape(T, TOP_K)
        flat_p = top_p.reshape(T, TOP_K)
        gate = jnp.zeros((T, E), dtype=flat_p.dtype)
        gate = gate.at[jnp.arange(T)[:, None], flat_i].add(flat_p)
        acc = jnp.maximum(jnp.sum(gate, axis=-1), EPS)
        out = jnp.zeros_like(x)
        for e in range(E):
            out = out + x @ expert_w[e] * gate[:, e:e + 1]
        out = (out / acc[:, None]).reshape(B, S, H)
        out = out + EPS * jnp.sum(top_p, axis=-1, keepdims=True)
        return out
    x = _layernorm(x + _L0_attn_ref(x, L0_attn_W_attn, L0_attn_W_proj), axis=-1)
    x = _layernorm(x + _L0_xattn_ref(x, ctx_1024, ctx_1024, L0_xattn_WQ, L0_xattn_WK, L0_xattn_WV, L0_xattn_WO, L0_xattn_bO), axis=-1)
    x = _layernorm(x + _L0_ffn_ref(x, L0_ffn_router_w, L0_ffn_router_b, L0_ffn_expert_w), axis=-1)
    return x

_drawn_inputs = setup_inputs


def setup_inputs(seed=0):
    import zlib

    import numpy as np

    out = dict(_drawn_inputs(seed))
    spreads = {'L0_xattn_bO': (0.0, 0.1)}
    factors = {}
    for name, (base, spread) in spreads.items():
        noise = np.random.default_rng([zlib.crc32(name.encode()), seed]).standard_normal(out[name].shape)
        drawn = base * np.exp(spread * noise) if base else spread * noise
        out[name] = jnp.asarray(drawn.astype(out[name].dtype))
    for name, factor in factors.items():
        out[name] = (out[name] * factor).astype(out[name].dtype)
    return out
```

```python
from contextlib import ExitStack

import concourse.bass as bass
from concourse import mybir

P = 128
ALU = mybir.AluOpType
ACT = mybir.ActivationFunctionType
AX = mybir.AxisListType
F32 = mybir.dt.float32
F32R = mybir.dt.float32r

C = 128
T = 64
B = 128
H = 16
J = H // 2
E = 16
TOP = 6
NB = 4
NR = NB // 2
TOK = NB * T
NT = B // NB
HD = C // H
DK = 64
LN_EPS = 1e-5
TOP_EPS = 1e-10
GATE_STEPS = 20

K_IDENT = 0
K_CAUSAL = K_IDENT + P
K_VMASK = K_CAUSAL + T
K_QMASK = K_VMASK + C
K_KMASK = K_QMASK + J
K_COLS = K_KMASK + 2

JOBS = [
    ("Q", "G0", "l1"), ("K", "G1", "l1"), ("V", "M0", "l1"),
    ("S2_0", "S", "l2"),
    ("FF0", "G0", "ff"), ("FF1", "G1", "ff"), ("S1_0", "T0", "l1"),
    ("S2_1", "S", "l2"),
    ("Z0", "G1", "l1"), ("FF2", "G0", "ff"), ("Z1", "G1", "l1"), ("FF3", "G0", "ff"), ("S1_1", "T1", "l1"),
    ("Z2", "G1", "l1"), ("FF4", "G0", "ff"), ("Z3", "G1", "l1"), ("FF5", "G0", "ff"), ("S1_2", "T0", "l1"),
    ("Z4", "G1", "l1"), ("FF6", "G0", "ff"), ("Z5", "G1", "l1"), ("FF7", "G0", "ff"), ("S1_3", "T1", "l1"),
    ("Z6", "G1", "l1"), ("Z7", "G0", "l1"),
    ("PT0a", "T0", "l2"), ("PT0b", "T1", "l2"), ("VB0", "G1", "l1"), ("AC0", "", "l2"),
    ("PT1a", "T0", "l2"), ("PT1b", "T1", "l2"), ("VB1", "G0", "l1"), ("AC1", "M1", "l2"),
    ("VB2", "G1", "l1"), ("Y", "M0", "l1"), ("VB3", "G0", "l1"), ("VB4", "G1", "l1"),
    ("X2T", "M1", "l2"), ("VB5", "G0", "l1"), ("PR", "M0", "l1"), ("VB6", "G1", "l1"),
    ("LG", "M1", "l2"), ("VB7", "G0", "l1"), ("X1T", "M0", "l1"),
]
BANK = {job: bank for job, bank, _ in JOBS}
BANKS = ["G0", "G1", "S", "T0", "T1", "M0", "M1"]


def stages(turn):
    return {s for s, t in (("l1", turn + 1), ("l2", turn), ("ff", turn - 1)) if 0 <= t < NT}


def fills(bank, on, before=None):
    n = 0
    for job, b, stage in JOBS:
        if job == before:
            break
        n += b == bank and stage in on
    return n


ALL = {"l1", "l2", "ff"}


def earlier(turn, job):
    bank = BANK[job]
    first = fills(bank, stages(-1)) + fills(bank, stages(0))
    if isinstance(turn, int) and not 1 <= turn <= NT - 2:
        n = sum(fills(bank, stages(u)) for u in range(-1, turn))
        return n + fills(bank, stages(turn), job)
    return (turn - 1) * fills(bank, ALL) + (first + fills(bank, ALL, job))


def decoder(nc, x, x_t, ctx_t, w_attn, w_proj, wq_t, wk_t, wv_t, wo, b_o, router_t, router_b, expert_w, consts, out):
    ctx = ExitStack()
    with ctx:
        def sb(name, shape, dt=F32):
            return ctx.enter_context(nc.sbuf_tensor(name, shape, dt))

        def sem(name):
            return ctx.enter_context(nc.semaphore(name))

        ps = {}
        for b in BANKS:
            ps[b] = ctx.enter_context(nc.psum_tensor("ps_" + b, [P, 1024 if b == "S" else 512], F32))
        full = {b: sem("full_" + b) for b in BANKS}
        emptied = {b: sem("emptied_" + b) for b in BANKS}

        const = sb("const", [P, K_COLS])
        ident = const[:, K_IDENT:K_IDENT + P]
        causal = const[:, K_CAUSAL:K_CAUSAL + T]
        vmask = const[:, K_VMASK:K_VMASK + C]
        qmask = const[:, K_QMASK:K_QMASK + J]
        kmask = const[:, K_KMASK:K_KMASK + 2]
        w_attn_sb = sb("w_attn_sb", [P, 3 * C])
        w_proj_sb = sb("w_proj_sb", [P, 2, C])
        w_qk_hi, w_qk_lo = sb("w_qk_hi", [P, 2 * C], F32R), sb("w_qk_lo", [P, 2 * C], F32R)
        bo_sb = sb("bo_sb", [P, C])
        rb_sb = sb("rb_sb", [P, E])
        router_sb = sb("router_sb", [P, E])
        a_hi, a_lo = sb("a_hi", [P, H, C], F32R), sb("a_lo", [P, H, C], F32R)
        vo_hi, vo_lo = sb("vo_hi", [P, 2, J * C], F32R), sb("vo_lo", [P, 2, J * C], F32R)
        ex_hi, ex_lo = sb("ex_hi", [P, E * C], F32R), sb("ex_lo", [P, E * C], F32R)

        x_sb = sb("x_sb", [P, NR, C])
        xT = sb("xT", [P, NB, 2, T])
        cT = sb("cT", [P, TOK])
        xT_hi, xT_lo = sb("xT_hi", [P, TOK], F32R), sb("xT_lo", [P, TOK], F32R)
        cT_hi, cT_lo = sb("cT_hi", [P, TOK], F32R), sb("cT_lo", [P, TOK], F32R)
        qm = sb("qm", [P, NB, J, T])
        kp = sb("kp", [P, NB, 2, T])
        vp = sb("vp", [P, NB, J, 32])
        relu = sb("relu", [P, 2, J * T])
        allowed = sb("allowed", [P, J * T])
        poly = sb("poly", [P, J * T])
        p1 = sb("p1", [P, NB, J * T])
        yT = sb("yT", [P, 2, TOK])
        r1 = sb("r1", [P, NR, C])
        x1 = sb("x1", [P, NR, C])
        x1b = sb("x1b", [P, NR, C])
        x1T = sb("x1T", [P, TOK])
        z = sb("z", [P, NB, H, T])
        p2 = sb("p2", [P, NR, H * T])
        p2T = sb("p2T", [P, NR, J, P])
        vb_raw = sb("vb_raw", [P, NR, 2, J * C])
        vb = sb("vb", [P, NB, J * C])
        r2 = sb("r2", [P, NR, C])
        x2 = sb("x2", [P, NR, C])
        x2T = sb("x2T", [P, TOK])
        x2T_hi, x2T_lo = sb("x2T_hi", [P, TOK], F32R), sb("x2T_lo", [P, TOK], F32R)
        weighted = sb("weighted", [P, NR, E * C])
        r3 = sb("r3", [P, NR, C])
        x3 = sb("x3", [P, NR, C])
        rowmax, rowsum, rowinv = sb("rowmax", [P, NR, H]), sb("rowsum", [P, NR, H]), sb("rowinv", [P, NR, H])
        stats, mv, rstd = sb("stats", [P, 3, NR, 6]), sb("mv", [P, 3, NR, 2]), sb("rstd", [P, 3, NR])
        power, one, scratch = sb("power", [P, NR]), sb("one", [P, 1]), sb("scratch", [P, 1])
        logit = sb("logit", [P, NR, E])
        lmax, lsum, linv = sb("lmax", [P, NR]), sb("lsum", [P, NR]), sb("linv", [P, NR])
        prob, left = sb("prob", [P, NR, E + 2]), sb("left", [P, NR, E + 2])
        best = sb("best", [P, NR, 8])
        gate = sb("gate", [P, NR, E])
        tsum, tinv = sb("tsum", [P, NR]), sb("tinv", [P, NR])
        gsum, ginv, geps = sb("gsum", [P, NR]), sb("ginv", [P, NR]), sb("geps", [P, NR])

        wq_ld, wk_ld = weighted[:, 0, 0:J * C], weighted[:, 0, J * C:2 * J * C]
        wv_ld, wo_ld = weighted[:, 1, 0:J * C], weighted[:, 1, J * C:2 * J * C]
        ex_ld = z[:].rearrange("p b h t -> p (b h t)")[:, 0:E * C]

        w_in, expert_in = sem("w_in"), sem("expert_in")
        zeroed, power_set = sem("zeroed"), sem("power_set")
        product_ready, product_hi, product_read = sem("product_ready"), sem("product_hi"), sem("product_read")
        weights_hi, weights_split = sem("weights_hi"), sem("weights_split")
        x_in, xT_in, cT_in = sem("x_in"), sem("xT_in"), sem("cT_in")
        xT_hi_ready, xT_split = sem("xT_hi_ready"), sem("xT_split")
        cT_hi_ready, cT_split = sem("cT_hi_ready"), sem("cT_split")
        relu_ready, square_ready, allowed_ready, p1_ready = sem("relu_ready"), sem("square_ready"), sem("allowed_ready"), sem("p1_ready")
        x1_ready, x1b_ready = sem("x1_ready"), sem("x1b_ready")
        vb_in = sem("vb_in")
        rowmax_ready, exp_ready, rowsum_ready, rowinv_ready, p2_ready = sem("rowmax_ready"), sem("exp_ready"), sem("rowsum_ready"), sem("rowinv_ready"), sem("p2_ready")
        x2_ready, x2T_hi_ready, x2T_split = sem("x2_ready"), sem("x2T_hi_ready"), sem("x2T_split")
        logit_exp_ready, gate_steps = sem("logit_exp_ready"), sem("gate_steps")
        weighted_ready, add_steps = sem("weighted_ready"), sem("add_steps")
        r3_ready, x3_ready, out_done = sem("r3_ready"), sem("x3_ready"), sem("out_done")
        ln_stats, ln_var, ln_eps, ln_rstd = ([sem(f"ln{n}_{what}") for n in (1, 2, 3)] for what in ("stats", "var", "eps", "rstd"))

        N_SETUP = 2 * H // 4

        def wait(eng, s, n):
            if not (isinstance(n, int) and n == 0):
                eng.wait_ge(s, n)

        def wait_full(eng, turn, job):
            wait(eng, full[BANK[job]], earlier(turn, job) + 1)

        def wait_emptied(eng, turn, job):
            wait(eng, emptied[BANK[job]], earlier(turn, job) + 1)

        def turns(eng, body):
            for i in (-1, 0, 1):
                body(i)
            with eng.Fori(2, NT - 2) as i:
                body(i)
            for i in range(NT - 2, NT + 1):
                body(i)

        def product_hi_part(n):
            what, par, q = n // 4, n % 2, n // 2 % 2
            src = ps[("G0", "G1")[par]][:].rearrange("p (j c) -> p j c", j=4)
            if what == 0:
                return a_hi[:].rearrange("p (j e) c -> p e j c", e=2)[:, par, 4 * q:4 * q + 4], src, float(DK) ** -0.5
            return vo_hi[:, par, 512 * q:512 * q + 512].rearrange("p (j c) -> p j c", j=4), src, 1.0

        def product_lo_part(n):
            what, par, q = n // 4, n % 2, n // 2 % 2
            if what == 0:
                return a_lo[:].rearrange("p (j e) c -> p e j c", e=2)[:, par, 4 * q:4 * q + 4]
            return vo_lo[:, par, 512 * q:512 * q + 512].rearrange("p (j c) -> p j c", j=4)

        def on(turn):
            return stages(turn) if isinstance(turn, int) else ALL

        tile_x = x.rearrange("(t r h) s c -> t (h s) r c", r=NR, h=2)
        tile_out = out.rearrange("(t r h) s c -> t (h s) r c", r=NR, h=2)

        def at(ap, t):
            return ap[bass.ds(t, 1)][0]

        block = ctx.enter_context(nc.Block())

        @block.sync
        def _(sp):
            for dst, src in ((const[:], consts), (w_attn_sb[:], w_attn), (wq_ld, wq_t), (wk_ld, wk_t), (wv_ld, wv_t),
                             (wo_ld.rearrange("p (j c) -> p j c", j=J), wo.rearrange("(j p) c -> p j c", p=P)),
                             (router_sb[:], router_t),
                             (bo_sb[:], b_o.partition_broadcast(P)), (rb_sb[:], router_b.partition_broadcast(P))):
                sp.dma_start(dst, src).then_inc(w_in, 16)
            sp.wait_ge(zeroed, 1)
            for g in range(4):
                sp.dma_start(w_proj_sb[32 * g:32 * g + 16], w_proj.rearrange("(a g c) n -> g c a n", a=2, g=4)[g]).then_inc(w_in, 16)
            sp.dma_start(ex_ld.rearrange("p (e n) -> p e n", e=E), expert_w.rearrange("e p n -> p e n")).then_inc(expert_in, 16)

            def load(t):
                sp.dma_start(cT[:], at(ctx_t, t)).then_inc(cT_in, 16)
                sp.dma_start(xT[:], at(x_t, t)).then_inc(xT_in, 16)

            def load_x(t):
                sp.dma_start(x_sb[:], at(tile_x, t)).then_inc(x_in, 16)

            load(0)
            load_x(0)

            def body(i):
                t = i + 1
                more = not isinstance(i, int) or t + 1 < NT
                if "l1" in on(i) and more:
                    sp.wait_ge(cT_split, t + 1)
                    sp.wait_ge(xT_split, t + 1)
                    wait_full(sp, i, "V")
                    load(t + 1)
                if "ff" in on(i):
                    sp.wait_ge(x3_ready, NR * i)
                    sp.dma_start(at(tile_out, i - 1), x3[:]).then_inc(out_done, 16)
                if "l1" in on(i):
                    if more:
                        wait_emptied(sp, i, "PR")
                        load_x(t + 1)
                    wait_emptied(sp, i, "VB7")
                    if "l2" in on(i):
                        wait_full(sp, i, "AC1")
                    for half in range(2):
                        for par in range(2):
                            sp.dma_start(vb[64 * par:64 * par + 64].rearrange("p (r h) n -> p r h n", h=2)[:, :, half],
                                         vb_raw[64 * half:64 * half + 64, :, par]).then_inc(vb_in, 16)

            turns(sp, body)
            sp.wait_ge(out_done, 16 * NT)

        @block.tensor
        def _(pe):
            def mm(o, l, r, start=True, stop=True):
                return pe.matmul(o, l, r, start=start, stop=stop)

            def mm3(o, l_hi, l_lo, r_hi, r_lo):
                mm(o, l_hi, r_hi, True, False)
                mm(o, l_hi, r_lo, False, False)
                return mm(o, l_lo, r_hi, False, True)

            pe.wait_ge(w_in, 16 * 13)
            for n in range(N_SETUP):
                what, par, q = n // 4, n % 2, n // 2 % 2
                rows = slice(64 * par, 64 * par + 64)
                left_w, right_w = ((wk_ld, wq_ld), (wv_ld, wo_ld))[what]
                if n >= 2:
                    pe.wait_ge(product_read, n - 1)
                for k in range(4):
                    j = 4 * q + k
                    cols = slice(C * j, C * j + C)
                    last = mm(ps[("G0", "G1")[par]][:, C * k:C * k + C], left_w[rows, cols], right_w[rows, cols])
                last.then_inc(product_ready, 1)
            pe.wait_ge(product_read, N_SETUP)
            pe.wait_ge(weights_split, 2)

            def body(i):
                t = i + 1
                tf = i - 1

                def q():
                    pe.wait_ge(xT_split, t + 1)
                    return mm3(ps["G0"][:, 0:TOK], w_qk_hi[:, 0:C], w_qk_lo[:, 0:C], xT_hi[:], xT_lo[:])

                def k():
                    return mm3(ps["G1"][:, 0:TOK], w_qk_hi[:, C:2 * C], w_qk_lo[:, C:2 * C], xT_hi[:], xT_lo[:])

                def v():
                    pe.wait_ge(xT_in, 16 * (t + 1))
                    for b in range(NB):
                        last = mm(ps["M0"][:, C * b:C * b + C], xT[:, b].rearrange("p a t -> p (a t)"), w_attn_sb[:, 2 * C:3 * C])
                    return last

                def s1(b):
                    wait_emptied(pe, i, "Q")
                    wait_emptied(pe, i, "K")
                    return mm(ps[("T0", "T1")[b % 2]][:], kp[:, b].rearrange("p a t -> p (a t)"), qm[:, b].rearrange("p j t -> p (j t)"))

                def y():
                    wait_emptied(pe, i, "V")
                    pe.wait_ge(p1_ready, NB * (t + 1))
                    out_y = ps["M0"][:].rearrange("p (a n) -> p a n", a=2)
                    for b in range(NB):
                        for j in range(J):
                            a, g = j // 4, j % 4
                            last = mm(out_y[32 * g:32 * g + 32, a, T * b:T * b + T], vp[:, b, j], p1[:, b, T * j:T * j + T])
                    return last

                def pr():
                    wait_emptied(pe, i, "Y")
                    for r in range(NR):
                        for a in range(2):
                            last = mm(ps["M0"][:, C * r:C * r + C], yT[:, a, P * r:P * r + P], w_proj_sb[:, a], a == 0, a == 1)
                    return last

                def x1_turn():
                    pe.wait_ge(x1_ready, NR * (t + 1))
                    for r in range(NR):
                        last = pe.transpose(ps["M0"][:, P * r:P * r + P], x1[:, r], ident)
                    return last

                def z_heads(n):
                    pe.wait_ge(cT_split, t + 1)
                    for k in range(2):
                        last = mm3(ps[BANK[f"Z{n}"]][:, TOK * k:TOK * k + TOK], a_hi[:, 2 * n + k], a_lo[:, 2 * n + k], cT_hi[:], cT_lo[:])
                    return last

                def vb_part(n):
                    r, par, q = n // 4, n // 2 % 2, n % 2
                    cols, rows = slice(512 * q, 512 * q + 512), slice(P * r, P * r + P)
                    return mm3(ps[BANK[f"VB{n}"]][:], cT_hi[:, rows], cT_lo[:, rows], vo_hi[:, par, cols], vo_lo[:, par, cols])

                def s2(r):
                    wait_emptied(pe, i - 1, "X1T")
                    wait_emptied(pe, i - 1, "Z7")
                    for q in range(2):
                        for h in range(2):
                            b = 2 * r + h
                            last = mm(ps["S"][64 * h:64 * h + 64, 512 * q:512 * q + 512], x1T[:, T * b:T * b + T],
                                      z[:, b, 8 * q:8 * q + 8].rearrange("p h t -> p (h t)"))
                    return last

                def p2_turn(r, q):
                    pe.wait_ge(p2_ready, NR * i + r + 1)
                    for k in range(4):
                        j = 4 * q + k
                        last = pe.transpose(ps[("T0", "T1")[q]][:, P * k:P * k + P], p2[:, r, P * j:P * j + P], ident)
                    return last

                def ac(r):
                    pe.wait_ge(vb_in, 64 * (i + 1))
                    wait_emptied(pe, i, f"PT{r}b")
                    for j in range(J):
                        for h in range(2):
                            last = mm(ps["M1"][64 * h:64 * h + 64, C * r:C * r + C], p2T[:, r, j, T * h:T * h + T],
                                      vb[:, 2 * r + h, C * j:C * j + C], j == 0, j == J - 1)
                    return last

                def x2_turn():
                    pe.wait_ge(x2_ready, NR * (i + 1))
                    for r in range(NR):
                        last = pe.transpose(ps["M1"][:, P * r:P * r + P], x2[:, r], ident)
                    return last

                def lg():
                    wait_emptied(pe, i, "X2T")
                    for r in range(NR):
                        last = mm(ps["M1"][:, E * r:E * r + E], x2T[:, P * r:P * r + P], router_sb[:])
                    return last

                def ff(n):
                    pe.wait_ge(x2T_split, tf + 1)
                    r, q = n // 4, n % 4
                    rows, cols = slice(P * r, P * r + P), slice(512 * q, 512 * q + 512)
                    return mm3(ps[BANK[f"FF{n}"]][:], x2T_hi[:, rows], x2T_lo[:, rows], ex_hi[:, cols], ex_lo[:, cols])

                work = {"Q": q, "K": k, "V": v, "Y": y, "PR": pr, "X1T": x1_turn, "X2T": x2_turn, "LG": lg,
                        "S2_0": lambda: s2(0), "S2_1": lambda: s2(1), "AC0": lambda: ac(0), "AC1": lambda: ac(1),
                        "PT0a": lambda: p2_turn(0, 0), "PT0b": lambda: p2_turn(0, 1),
                        "PT1a": lambda: p2_turn(1, 0), "PT1b": lambda: p2_turn(1, 1)}
                for job, bank, stage in JOBS:
                    if stage not in on(i):
                        continue
                    if job == "AC0":
                        wait(pe, emptied["M1"], earlier(i, "AC1"))
                    elif job != "AC1":
                        wait(pe, emptied[bank], earlier(i, job))
                    if job in work:
                        last = work[job]()
                    elif job[0] == "Z":
                        last = z_heads(int(job[1:]))
                    elif job[:2] == "VB":
                        last = vb_part(int(job[2:]))
                    elif job[:2] == "S1":
                        last = s1(int(job[3:]))
                    else:
                        last = ff(int(job[2:]))
                    if bank:
                        last.then_inc(full[bank], 1)

            turns(pe, body)

        @block.scalar
        def _(act):
            def copy(dst, src, scale=1.0):
                return nc.scalar.activation(dst, src, ACT.Copy, scale=scale)

            act.wait_ge(w_in, 16 * 13)
            copy(w_qk_hi[:], w_attn_sb[:, 0:2 * C]).then_inc(weights_hi, 1)
            for n in range(N_SETUP):
                act.wait_ge(product_ready, n + 1)
                copy(*product_hi_part(n)).then_inc(product_hi, 1)
            act.wait_ge(expert_in, 16)
            copy(ex_hi[:], ex_ld).then_inc(weights_hi, 1)

            def body(i):
                t = i + 1

                def exp(r):
                    wait_emptied(act, i, f"S2_{r}")
                    nc.scalar.activation(p2[:, r], p2[:, r], ACT.Exp).then_inc(exp_ready, 1)

                def relu_square(b):
                    wait_full(act, i, f"S1_{b}")
                    nc.scalar.activation(relu[:, b % 2], ps[BANK[f"S1_{b}"]][:], ACT.Relu).then_inc(relu_ready, 1)
                    act.wait_ge(relu_ready, NB * t + b + 1)
                    nc.scalar.activation(relu[:, b % 2], relu[:, b % 2], ACT.Square).then_inc(square_ready, 1)

                def move(job, dst, src, scale=1.0):
                    wait_full(act, i, job)
                    copy(dst, src, scale).then_inc(emptied[BANK[job]], 1)

                def move_z(n):
                    bank = ps[BANK[f"Z{n}"]][:].rearrange("p (h b t) -> p h b t", h=2, b=NB)
                    move(f"Z{n}", z[:, :, 2 * n:2 * n + 2].rearrange("p b h t -> p h b t"), bank)

                def move_p2T(r, q):
                    job = f"PT{r}" + "ab"[q]
                    move(job, p2T[:, r, 4 * q:4 * q + 4].rearrange("p j n -> p (j n)"), ps[BANK[job]][:])

                def move_vb(n):
                    if n == 0:
                        wait(act, vb_in, 64 * t)
                    r, par, q = n // 4, n // 2 % 2, n % 2
                    move(f"VB{n}", vb_raw[:, r, par, 512 * q:512 * q + 512], ps[BANK[f"VB{n}"]][:])

                l1, l2 = "l1" in on(i), "l2" in on(i)
                if l1:
                    wait_full(act, i, "K")
                    keys = ps["G1"][:, 0:TOK].rearrange("p (b t) -> p b t", b=NB)
                    copy(kp[:, :, 0], keys, kmask[:, 0:1])
                    copy(kp[:, :, 1], keys, kmask[:, 1:2]).then_inc(emptied["G1"], 1)
                if l2:
                    exp(0)
                if l1:
                    relu_square(0)
                if l2:
                    exp(1)
                if l1:
                    for n in range(8):
                        move_z(n)
                        if n in (1, 3, 5):
                            relu_square(n // 2 + 1)
                if l2:
                    move_p2T(0, 0)
                    move_p2T(0, 1)
                if l1:
                    move_vb(0)
                if l2:
                    move_p2T(1, 0)
                    move_p2T(1, 1)
                if l1:
                    move_vb(1)
                    move_vb(2)
                    move("Y", yT[:].rearrange("p a n -> p (a n)"), ps["M0"][:], 1e-3)
                    move_vb(3)
                    move_vb(4)
                if l2:
                    move("X2T", x2T[:], ps["M1"][:, 0:TOK])
                if l1:
                    move_vb(5)
                    move_vb(6)
                    move_vb(7)
                    move("X1T", x1T[:], ps["M0"][:, 0:TOK])
                if l2:
                    act.wait_ge(gate_steps, GATE_STEPS * i + 2)
                    nc.scalar.activation(logit[:], logit[:], ACT.Exp).then_inc(logit_exp_ready, 1)

            turns(act, body)

        @block.vector
        def _(dve):
            V = nc.vector
            V.memset(w_proj_sb[:], 0.0).then_inc(zeroed, 1)
            V.memset(vp[:], 0.0)
            V.memset(prob[:], -1.0).then_inc(zeroed, 1)
            dve.wait_ge(zeroed, 2)
            dve.wait_ge(w_in, 16 * 13)
            dve.wait_ge(weights_hi, 1)
            V.tensor_tensor(w_qk_lo[:], w_attn_sb[:, 0:2 * C], w_qk_hi[:].bitcast(F32), ALU.subtract).then_inc(weights_split, 1)
            for n in range(N_SETUP):
                dve.wait_ge(product_hi, n + 1)
                hi, src, scale = product_hi_part(n)
                V.scalar_tensor_tensor(product_lo_part(n), src, scale, hi.bitcast(F32), ALU.mult, ALU.subtract).then_inc(product_read, 1)
            dve.wait_ge(weights_hi, 2)
            V.tensor_tensor(ex_lo[:], ex_ld, ex_hi[:].bitcast(F32), ALU.subtract).then_inc(weights_split, 1)

            def body(i):
                t, f = i + 1, i - 1

                def hold_wait():
                    V.memset(scratch[:], 0.0)

                def layernorm(n, tile, src, dst, done, src_ready):
                    k = n - 1
                    src_ready()
                    for r in range(NR):
                        V.bn_stats(stats[:, k, r], src[:, r]).then_inc(ln_stats[k], 1)
                    dve.wait_ge(ln_stats[k], NR * (tile + 1))
                    hold_wait()
                    for r in range(NR):
                        V.bn_aggr(mv[:, k, r], stats[:, k, r]).then_inc(ln_var[k], 1)
                    dve.wait_ge(ln_var[k], NR * (tile + 1))
                    V.tensor_scalar(rstd[:, k], mv[:, k, :, 1], LN_EPS, None, ALU.add).then_inc(ln_eps[k], 1)
                    dve.wait_ge(ln_rstd[k], tile + 1)
                    for r in range(NR):
                        V.tensor_scalar(dst[:, r], src[:, r], mv[:, k, r, 0:1], rstd[:, k, r:r + 1], ALU.subtract, ALU.mult).then_inc(done, 1)

                def row_max(r):
                    wait_full(dve, i, f"S2_{r}")
                    scores = ps["S"][:].rearrange("p (h k) -> p h k", h=H)
                    V.tensor_reduce(rowmax[:, r], scores, AX.X, ALU.max).then_inc(rowmax_ready, 1)
                    dve.wait_ge(rowmax_ready, NR * i + r + 1)
                    V.tensor_tensor(p2[:, r].rearrange("p (h k) -> p h k", h=H), scores,
                                    rowmax[:, r].unsqueeze(2).broadcast_to([P, H, T]), ALU.subtract).then_inc(emptied["S"], 1)

                def row_sum(r):
                    dve.wait_ge(exp_ready, NR * i + r + 1)
                    V.tensor_reduce(rowsum[:, r], p2[:, r].rearrange("p (h k) -> p h k", h=H), AX.X, ALU.add).then_inc(rowsum_ready, 1)
                    dve.wait_ge(rowsum_ready, NR * i + r + 1)
                    V.reciprocal(rowinv[:, r], rowsum[:, r]).then_inc(rowinv_ready, 1)

                def polymax(b):
                    bank, name = ps[BANK[f"S1_{b}"]][:], BANK[f"S1_{b}"]
                    wait(dve, p1_ready, NB * t + b)
                    dve.wait_ge(relu_ready, NB * t + b + 1)
                    V.scalar_tensor_tensor(allowed[:].rearrange("p (j n) -> p j n", j=J), bank.rearrange("p (j n) -> p j n", j=J), -100.0,
                                           causal.unsqueeze(1).broadcast_to([P, J, T]), ALU.is_ge, ALU.mult).then_inc(allowed_ready, 1)
                    dve.wait_ge(square_ready, NB * t + b + 1)
                    V.scalar_tensor_tensor(poly[:], bank, -0.01, relu[:, b % 2], ALU.mult, ALU.max).then_inc(emptied[name], 1)
                    dve.wait_ge(allowed_ready, NB * t + b + 1)
                    wait_emptied(dve, i, f"S1_{b}")
                    V.scalar_tensor_tensor(p1[:, b], poly[:], 1.0, allowed[:], ALU.add, ALU.mult).then_inc(p1_ready, 1)

                def weigh(n):
                    r, q = n // 4, n % 4
                    job = f"FF{n}"
                    wait_full(dve, i, job)
                    if n == 0:
                        dve.wait_ge(gate_steps, GATE_STEPS * (f + 1))
                        wait(dve, add_steps, 8 * f)
                    V.tensor_tensor(weighted[:, r, 512 * q:512 * q + 512].rearrange("p (e c) -> p e c", e=4),
                                    ps[BANK[job]][:].rearrange("p (e c) -> p e c", e=4),
                                    gate[:, r, 4 * q:4 * q + 4].unsqueeze(2).broadcast_to([P, 4, C]), ALU.mult).then_inc(emptied[BANK[job]], 1)

                def gates():
                    count = [0]

                    def step(ins):
                        count[0] += 1
                        ins.then_inc(gate_steps, 1)
                        dve.wait_ge(gate_steps, GATE_STEPS * i + count[0])

                    wait_full(dve, i, "LG")
                    V.tensor_tensor(logit[:], ps["M1"][:, 0:NR * E].rearrange("p (r e) -> p r e", r=NR),
                                    rb_sb[:].unsqueeze(1).broadcast_to([P, NR, E]), ALU.add).then_inc(emptied["M1"], 1)
                    wait_emptied(dve, i, "LG")
                    step(V.tensor_reduce(lmax[:], logit[:], AX.X, ALU.max))
                    step(V.tensor_tensor(logit[:], logit[:], lmax[:].unsqueeze(2).broadcast_to([P, NR, E]), ALU.subtract))
                    dve.wait_ge(logit_exp_ready, i + 1)
                    step(V.tensor_reduce(lsum[:], logit[:], AX.X, ALU.add))
                    step(V.reciprocal(linv[:], lsum[:]))
                    step(V.tensor_tensor(prob[:, :, 0:E], logit[:], linv[:].unsqueeze(2).broadcast_to([P, NR, E]), ALU.mult))
                    hold_wait()
                    step(V.max(best[:, 0], prob[:, 0, 0:E]))
                    hold_wait()
                    step(V.max(best[:, 1], prob[:, 1, 0:E]))
                    step(V.tensor_reduce(tsum[:], best[:, :, 0:TOP], AX.X, ALU.add))
                    step(V.tensor_scalar(tsum[:], tsum[:], TOP_EPS, None, ALU.add))
                    step(V.reciprocal(tinv[:], tsum[:]))
                    step(V.memset(best[:, :, TOP:8], -1.0))
                    for r in range(NR):
                        hold_wait()
                        step(V.match_replace(left[:, r], best[:, r], prob[:, r], 0.0))
                    step(V.tensor_tensor(gate[:], prob[:, :, 0:E], left[:, :, 0:E], ALU.subtract))
                    step(V.tensor_tensor(gate[:], gate[:], tinv[:].unsqueeze(2).broadcast_to([P, NR, E]), ALU.mult))
                    step(V.tensor_reduce(gsum[:], gate[:], AX.X, ALU.add))
                    step(V.tensor_scalar(geps[:], gsum[:], TOP_EPS, None, ALU.mult))
                    step(V.tensor_scalar(gsum[:], gsum[:], TOP_EPS, None, ALU.max))
                    step(V.reciprocal(ginv[:], gsum[:]))
                    step(V.tensor_tensor(gate[:], gate[:], ginv[:].unsqueeze(2).broadcast_to([P, NR, E]), ALU.mult))
                    assert count[0] == GATE_STEPS, count[0]

                l1, l2, ff = ("l1" in on(i)), ("l2" in on(i)), ("ff" in on(i))
                if l1:
                    wait_full(dve, i, "Q")
                    V.tensor_tensor(qm[:], ps["G0"][:, 0:TOK].rearrange("p (b t) -> p b t", b=NB).unsqueeze(2).broadcast_to([P, NB, J, T]),
                                    qmask.unsqueeze(1).unsqueeze(3).broadcast_to([P, NB, J, T]), ALU.mult).then_inc(emptied["G0"], 1)
                    wait_full(dve, i, "V")
                    V.tensor_tensor(vp[:, :, :, 0:16], ps["M0"][:].rearrange("p (b j c) -> p b j c", b=NB, j=J),
                                    vmask.rearrange("p (j c) -> p j c", j=J).unsqueeze(1).broadcast_to([P, NB, J, 16]), ALU.mult).then_inc(emptied["M0"], 1)
                if l2:
                    row_max(0)
                if ff:
                    weigh(0)
                    weigh(1)
                if l2:
                    row_sum(0)
                if l1:
                    polymax(0)
                if l2:
                    row_max(1)
                for n in range(2, 8):
                    if ff:
                        weigh(n)
                    if n == 4 and l2:
                        row_sum(1)
                    if l1 and n % 2:
                        polymax(n // 2)
                if ff:
                    for r in range(NR):
                        dve.wait_ge(add_steps, 8 * f + 4 * (r + 1))
                        V.scalar_tensor_tensor(r3[:, r], weighted[:, r, 0:C], geps[:, r:r + 1], x2[:, r], ALU.add, ALU.add).then_inc(r3_ready, 1)
                if l2:
                    wait_full(dve, i, "AC1")
                    dve.wait_ge(x1b_ready, i + 1)
                    V.tensor_tensor(r2[:].rearrange("p r c -> p (r c)"), ps["M1"][:, 0:NR * C], x1b[:].rearrange("p r c -> p (r c)"), ALU.add).then_inc(emptied["M1"], 1)
                    layernorm(2, i, r2, x2, x2_ready, lambda: wait_emptied(dve, i, "AC1"))
                if ff:
                    wait(dve, out_done, 16 * f)
                    layernorm(3, f, r3, x3, x3_ready, lambda: dve.wait_ge(r3_ready, NR * (f + 1)))
                if l1:
                    wait_full(dve, i, "PR")
                    dve.wait_ge(x_in, 16 * (t + 1))
                    V.tensor_tensor(r1[:].rearrange("p r c -> p (r c)"), ps["M0"][:, 0:NR * C], x_sb[:].rearrange("p r c -> p (r c)"), ALU.add).then_inc(emptied["M0"], 1)
                    layernorm(1, t, r1, x1, x1_ready, lambda: wait_emptied(dve, i, "PR"))
                if l2:
                    gates()

            turns(dve, body)

        @block.gpsimd
        def _(pool):
            G = nc.gpsimd
            G.memset(one[:], 1.0)
            G.memset(power[:], -0.5).then_inc(power_set, 1)
            pool.wait_ge(power_set, 1)

            def split(hi, lo, src, hi_ready, done, n):
                G.tensor_tensor(hi, src, one[:].unsqueeze(1).broadcast_to([P, NB, T]), ALU.mult).then_inc(hi_ready, 1)
                pool.wait_ge(hi_ready, n)
                G.tensor_tensor(lo, src, hi.bitcast(F32), ALU.subtract).then_inc(done, 1)

            x_columns = [xT_hi[:].rearrange("p (b t) -> p b t", b=NB), xT_lo[:].rearrange("p (b t) -> p b t", b=NB), xT[:, :, 0]]
            c_columns, x2_columns = ([a[:].rearrange("p (b t) -> p b t", b=NB) for a in three] for three in ((cT_hi, cT_lo, cT), (x2T_hi, x2T_lo, x2T)))
            pool.wait_ge(xT_in, 16)
            split(*x_columns, xT_hi_ready, xT_split, 1)

            def body(i):
                t, f = i + 1, i - 1
                l1, l2, ff = ("l1" in on(i)), ("l2" in on(i)), ("ff" in on(i))

                def root(n, tile):
                    pool.wait_ge(ln_eps[n - 1], tile + 1)
                    G.tensor_tensor(rstd[:, n - 1], rstd[:, n - 1], power[:], ALU.pow).then_inc(ln_rstd[n - 1], 1)

                if l1:
                    pool.wait_ge(cT_in, 16 * (t + 1))
                    if not (isinstance(i, int) and t == 0):
                        wait_full(pool, i - 1, "VB7")
                    split(*c_columns, cT_hi_ready, cT_split, t + 1)
                if l2:
                    for r in range(NR):
                        pool.wait_ge(rowinv_ready, NR * i + r + 1)
                        weights = p2[:, r].rearrange("p (h k) -> p h k", h=H)
                        G.tensor_tensor(weights, weights, rowinv[:, r].unsqueeze(2).broadcast_to([P, H, T]), ALU.mult).then_inc(p2_ready, 1)
                if ff:
                    for r in range(NR):
                        wait_emptied(pool, i, f"FF{4 * r + 3}")
                        for k, width in enumerate((8, 4, 2, 1)):
                            a, b = weighted[:, r, 0:width * C], weighted[:, r, width * C:2 * width * C]
                            G.tensor_tensor(a, a, b, ALU.add).then_inc(add_steps, 1)
                            if width > 1:
                                pool.wait_ge(add_steps, 8 * f + 4 * r + k + 1)
                if l2:
                    root(2, i)
                if ff:
                    root(3, f)
                if l2:
                    wait_emptied(pool, i, "X2T")
                    split(*x2_columns, x2T_hi_ready, x2T_split, i + 1)
                if l1:
                    root(1, t)
                    pool.wait_ge(x1_ready, NR * (t + 1))
                    G.tensor_tensor(x1b[:], x1[:], bo_sb[:].unsqueeze(1).broadcast_to([P, NR, C]), ALU.add).then_inc(x1b_ready, 1)
                    if not isinstance(i, int) or t + 1 < NT:
                        pool.wait_ge(xT_in, 16 * (t + 2))
                        wait_full(pool, i, "V")
                        split(*x_columns, xT_hi_ready, xT_split, t + 2)

            turns(pool, body)


def constants():
    import numpy as np
    p = np.arange(P)
    k = np.zeros((P, K_COLS), np.float32)
    k[:, K_IDENT:K_IDENT + P] = np.eye(P)
    k[:, K_CAUSAL:K_CAUSAL + T] = (p % T)[:, None] <= np.arange(T)[None, :]
    k[:, K_VMASK:K_VMASK + C] = (p // T)[:, None] == (p // HD % 2)[None, :]
    k[:, K_QMASK:K_QMASK + J] = ((p // (2 * HD))[:, None] == np.arange(J)[None, :]) * np.float32(HD ** -0.5)
    k[:, K_KMASK:K_KMASK + 2] = (p // HD % 2)[:, None] == np.arange(2)[None, :]
    return k


def kernel(x, ctx_1024, L0_attn_W_attn, L0_attn_W_proj, L0_xattn_WQ, L0_xattn_WK, L0_xattn_WV, L0_xattn_WO,
           L0_xattn_bO, L0_ffn_router_w, L0_ffn_router_b, L0_ffn_expert_w):
    import numpy as np
    import concourse.bacc as bacc
    from concourse.bass_utils import run_bass_kernel_spmd

    def columns(a):
        return np.asarray(a).reshape(NT, TOK, C).transpose(0, 2, 1)

    def by_pair(w):
        return np.asarray(w).T.reshape(J, P, C).transpose(1, 0, 2).reshape(P, J * C)

    twice = np.repeat(columns(x).reshape(NT, C, NB, 1, T), 2, axis=3)
    arrays = {
        "x": x, "x_t": twice, "ctx_t": columns(ctx_1024), "w_attn": L0_attn_W_attn, "w_proj": L0_attn_W_proj,
        "wq_t": by_pair(L0_xattn_WQ), "wk_t": by_pair(L0_xattn_WK), "wv_t": by_pair(L0_xattn_WV), "wo": L0_xattn_WO,
        "b_o": L0_xattn_bO, "router_t": np.asarray(L0_ffn_router_w).T, "router_b": L0_ffn_router_b,
        "expert_w": L0_ffn_expert_w, "consts": constants(),
    }
    arrays = {n: np.ascontiguousarray(a) for n, a in arrays.items()}
    nc = bacc.Bacc("TRN2", target_bir_lowering=False, num_devices=1)
    args = {n: nc.dram_tensor("in_" + n, a.shape, mybir.dt.from_np(a.dtype), kind="ExternalInput").ap() for n, a in arrays.items()}
    out = nc.dram_tensor("out_0", (B, T, C), F32, kind="ExternalOutput").ap()
    decoder(nc, out=out, **args)
    r = run_bass_kernel_spmd(nc, [{"in_" + n: a for n, a in arrays.items()}], core_ids=[0])
    return r.results[0]["out_0"]
```

```python
from contextlib import ExitStack

import concourse.bass as bass
from concourse import mybir

P = 128
ALU = mybir.AluOpType
ACT = mybir.ActivationFunctionType
AX = mybir.AxisListType
F32 = mybir.dt.float32
F32R = mybir.dt.float32r

C = 128
T = 64
B = 128
H = 16
J = H // 2
E = 16
TOP = 6
NB = 4
NR = NB // 2
TOK = NB * T
NT = B // NB
HD = C // H
DK = 64
LN_EPS = 1e-5
TOP_EPS = 1e-10
GATE_STEPS = 20
GEPS_STEP = 16
ADD_STEPS = 10

K_IDENT = 0
K_CAUSAL = K_IDENT + P
K_QMASK = K_CAUSAL + T
K_KMASK = K_QMASK + J
K_COLS = K_KMASK + 2

JOBS = [
    ("S2_0", "S", "l2"), ("Y", "B2", "l1"), ("K", "B1", "s1"), ("Q", "B0", "s1"), ("V", "B5", "s1"),
    ("PR", "B2", "l1"), ("S2_1", "S", "l2"), ("S1_0", "B4", "s1"), ("Z6", "B1", "l1"), ("Z7", "B2", "l1"),
    ("Z3", "B3", "l1"), ("VB0", "B1", "l1"), ("S1_1", "B0", "s1"), ("Z5", "B2", "l1"), ("VB7", "B1", "l1"),
    ("Z4", "B4", "l1"), ("VB2", "B2", "l1"), ("S1_2", "B5", "s1"), ("VB5", "B1", "l1"), ("PT0a", "B3", "l2"),
    ("PT0b", "B2", "l2"), ("Z1", "B4", "l1"), ("S1_3", "B1", "s1"), ("AC0", "", "l2"), ("PT1a", "B3", "l2"),
    ("PT1b", "B5", "l2"), ("VB1", "B4", "l1"), ("VB6", "B3", "l1"), ("Z2", "B0", "l1"), ("AC1", "B2", "l2"),
    ("VB3", "B0", "l1"), ("VB4", "B5", "l1"), ("FF0", "B2", "ff"), ("FF3", "B4", "ff"), ("X1T", "B5", "l1"),
    ("Z0", "B0", "l1"), ("FF5", "B2", "ff"), ("FF1", "B5", "ff"), ("X2T", "B1", "l2"), ("FF2", "B3", "ff"),
    ("FF6", "B0", "ff"), ("FF7", "B2", "ff"), ("LG", "B1", "l2"), ("FF4", "B4", "ff"),
]
BANK = {job: bank for job, bank, _ in JOBS}
BANKS = ["B0", "B1", "B2", "B3", "B4", "B5", "S"]

SP_ORDER = """
    x_columns place0 x_rows place1 context store
""".split()
ACT_ORDER = """
    Y K V exp0 relu0 Z6 square0 Z7 Z3 VB0 exp1 Z5 VB7 Z4 relu1 VB2 square1 relu2 VB5 PT0b PT0a Z1 square2
    relu3 PT1a PT1b VB1 Z2 base3 square3 VB3 VB4 X1T Z0 VB6 X2T logit_exp
""".split()
DVE_ORDER = """
    row_max0 gate2 less_max0 gate3 queries row_sum0 projected row_inv0 row_max1 gate4 less_max1 allow0 gate5
    pieces0 gate6 gate7 row_sum1 row_inv1 stats1 p1_0 gate8 var1 gate9 allow1 gate10 pieces1 p1_1 allow2
    eps1 pieces2 gate11 gate12 norm1 gate13 p1_2 stats3 allow3 var3 gate14 gate15 eps3 gate16 attended
    stats2 gate17 pieces3 gate18 var2 eps2 gate19 weigh0 norm2 weigh3 weigh5 weigh1 weigh2 norm3 p1_3 logits
    gate0 weigh7 weigh4 gate1 weigh6
""".split()
POOL_ORDER = """
    context_hi context_lo shares0 add1.0 shares1 add1.1 root1 add1.2 add1.3 add1.4 next_x_hi root2 root3
    bias_x1 add0.0 next_x_lo add0.1 x2_hi add0.2 add0.3 x2_lo add0.4
""".split()


def first_of(order, steps):
    return min(steps, key=order.index)


def last_of(order, steps):
    return max(steps, key=order.index)


def stages(turn):
    return {s for s, t in (("s1", turn + 2), ("l1", turn + 1), ("l2", turn), ("ff", turn - 1), ("out", turn - 2)) if 0 <= t < NT}


def fills(bank, on, before=None):
    n = 0
    for job, b, stage in JOBS:
        if job == before:
            break
        n += b == bank and stage in on
    return n


ALL = {"s1", "l1", "l2", "ff", "out"}


def earlier(turn, job):
    bank = BANK[job]
    first = sum(fills(bank, stages(u)) for u in range(-2, 1))
    if isinstance(turn, int) and not 1 <= turn <= NT - 3:
        return sum(fills(bank, stages(u)) for u in range(-2, turn)) + fills(bank, stages(turn), job)
    return (turn - 1) * fills(bank, ALL) + (first + fills(bank, ALL, job))


def decoder(nc, x, x_t, ctx_t, w_attn, w_proj, wq_t, wk_t, wv_t, wo, b_o, router_t, router_b, expert_w, consts, out):
    ctx = ExitStack()
    with ctx:
        def sb(name, shape, dt=F32):
            return ctx.enter_context(nc.sbuf_tensor(name, shape, dt))

        def sem(name):
            return ctx.enter_context(nc.semaphore(name))

        ps = {}
        for b in BANKS:
            ps[b] = ctx.enter_context(nc.psum_tensor("ps_" + b, [P, 1024 if b == "S" else 512], F32))
        full = {b: sem("full_" + b) for b in BANKS}
        emptied = {b: sem("emptied_" + b) for b in BANKS}

        const = sb("const", [P, K_COLS])
        ident = const[:, K_IDENT:K_IDENT + P]
        causal = const[:, K_CAUSAL:K_CAUSAL + T]
        qmask = const[:, K_QMASK:K_QMASK + J]
        kmask = const[:, K_KMASK:K_KMASK + 2]
        w_attn_sb = sb("w_attn_sb", [P, 3 * C])
        w_proj_sb = sb("w_proj_sb", [P, 2, C])
        w_qk_hi, w_qk_lo = sb("w_qk_hi", [P, 2 * C], F32R), sb("w_qk_lo", [P, 2 * C], F32R)
        bo_sb = sb("bo_sb", [P, C])
        rb_sb = sb("rb_sb", [P, E])
        router_sb = sb("router_sb", [P, E])
        a_hi, a_lo = sb("a_hi", [P, H, C], F32R), sb("a_lo", [P, H, C], F32R)
        vo_hi, vo_lo = sb("vo_hi", [P, 2, J * C], F32R), sb("vo_lo", [P, 2, J * C], F32R)
        ex_hi, ex_lo = sb("ex_hi", [P, E * C], F32R), sb("ex_lo", [P, E * C], F32R)

        x_sb = sb("x_sb", [P, NR, C])
        xT = sb("xT", [P, NB, 2, T])
        cT = sb("cT", [P, TOK])
        xT_hi, xT_lo = sb("xT_hi", [P, TOK], F32R), sb("xT_lo", [P, TOK], F32R)
        cT_hi, cT_lo = sb("cT_hi", [P, TOK], F32R), sb("cT_lo", [P, TOK], F32R)
        qm = sb("qm", [P, NB, J, T])
        kp = sb("kp", [P, NB, 2, T])
        vp = sb("vp", [P, NB, J, 32])
        relu = sb("relu", [P, 2, J * T])
        allowed = sb("allowed", [P, J * T])
        poly = sb("poly", [P, J * T])
        p1 = sb("p1", [P, NB, J * T])
        yT = sb("yT", [P, 2, TOK])
        r1 = sb("r1", [P, NR, C])
        x1 = sb("x1", [P, NR, C])
        x1b = sb("x1b", [P, NR, C])
        x1T = sb("x1T", [P, TOK])
        z = sb("z", [P, NB, H, T])
        p2 = sb("p2", [P, NR, H * T])
        p2T = sb("p2T", [P, NR, J, P])
        vb_raw = sb("vb_raw", [P, NR, 2, J * C])
        vb = sb("vb", [P, NB, J * C])
        r2 = sb("r2", [P, NR, C])
        x2 = sb("x2", [P, NR, C])
        x2T = sb("x2T", [P, TOK])
        x2T_hi, x2T_lo = sb("x2T_hi", [P, TOK], F32R), sb("x2T_lo", [P, TOK], F32R)
        weighted = sb("weighted", [P, NR, E * C])
        base3, r3 = sb("base3", [P, NR, C]), sb("r3", [P, NR, C])
        x3 = sb("x3", [P, NR, C])
        rowmax, rowsum, rowinv = sb("rowmax", [P, NR, H]), sb("rowsum", [P, NR, H]), sb("rowinv", [P, NR, H])
        stats, mv, rstd = sb("stats", [P, 3, NR, 6]), sb("mv", [P, 3, NR, 2]), sb("rstd", [P, 3, NR])
        power, one, scratch = sb("power", [P, NR]), sb("one", [P, 1]), sb("scratch", [P, GATE_STEPS])
        logit = sb("logit", [P, NR, E])
        lmax, lsum, linv = sb("lmax", [P, NR]), sb("lsum", [P, NR]), sb("linv", [P, NR])
        prob, left = sb("prob", [P, NR, E + 2]), sb("left", [P, NR, E + 2])
        best = sb("best", [P, NR, 8])
        gate = sb("gate", [P, NR, E])
        tsum, tinv = sb("tsum", [P, NR]), sb("tinv", [P, NR])
        gsum, ginv, geps = sb("gsum", [P, NR]), sb("ginv", [P, NR]), sb("geps", [P, NR])

        wq_ld, wk_ld = weighted[:, 0, 0:J * C], weighted[:, 0, J * C:2 * J * C]
        wv_ld, wo_ld = weighted[:, 1, 0:J * C], weighted[:, 1, J * C:2 * J * C]
        ex_ld = z[:].rearrange("p b h t -> p (b h t)")[:, 0:E * C]

        w_in, expert_in = sem("w_in"), sem("expert_in")
        zeroed, power_set = sem("zeroed"), sem("power_set")
        product_ready, product_hi, product_read = sem("product_ready"), sem("product_hi"), sem("product_read")
        weights_hi, weights_split = sem("weights_hi"), sem("weights_split")
        x_in, xT_in, cT_in = sem("x_in"), sem("xT_in"), sem("cT_in")
        xT_hi_ready, xT_split = sem("xT_hi_ready"), sem("xT_split")
        cT_hi_ready, cT_split = sem("cT_hi_ready"), sem("cT_split")
        relu_ready, square_ready, allowed_ready, p1_ready = sem("relu_ready"), sem("square_ready"), sem("allowed_ready"), sem("p1_ready")
        x1_ready, x1b_ready = sem("x1_ready"), sem("x1b_ready")
        vb_in = [sem(f"vb_in{r}") for r in range(NR)]
        rowmax_ready, exp_ready, rowsum_ready, rowinv_ready, p2_ready = sem("rowmax_ready"), sem("exp_ready"), sem("rowsum_ready"), sem("rowinv_ready"), sem("p2_ready")
        x2_ready, x2T_hi_ready, x2T_split = sem("x2_ready"), sem("x2T_hi_ready"), sem("x2T_split")
        logit_exp_ready, gate_steps = sem("logit_exp_ready"), sem("gate_steps")
        weighted_ready, add_steps = sem("weighted_ready"), sem("add_steps")
        base3_ready, x3_ready, out_done = sem("base3_ready"), sem("x3_ready"), sem("out_done")
        ln_stats, ln_var, ln_eps, ln_rstd = ([sem(f"ln{n}_{what}") for n in (1, 2, 3)] for what in ("stats", "var", "eps", "rstd"))

        N_SETUP = 2 * H // 4

        def wait(eng, s, n):
            if not (isinstance(n, int) and n == 0):
                eng.wait_ge(s, n)

        def wait_full(eng, turn, job):
            wait(eng, full[BANK[job]], earlier(turn, job) + 1)

        def wait_emptied(eng, turn, job):
            wait(eng, emptied[BANK[job]], earlier(turn, job) + 1)

        def run(turn, order, steps):
            for word in order:
                name = max((n for n in steps if word.startswith(n)), key=len)
                rest = word[len(name):]
                args = [int(a) if a.isdigit() else a for a in rest.split(".")] if rest else []
                stage, step = steps[name]
                if (stage if isinstance(stage, str) else stage(*args)) in on(turn):
                    step(*args)

        def turns(eng, body):
            for i in range(-2, 3):
                body(i)
            with eng.Fori(3, NT - 3) as i:
                body(i)
            for i in range(NT - 3, NT + 2):
                body(i)

        def product_hi_part(n):
            what, par, q = n // 4, n % 2, n // 2 % 2
            src = ps[("B0", "B1")[par]][:].rearrange("p (j c) -> p j c", j=4)
            if what == 0:
                return a_hi[:].rearrange("p (j e) c -> p e j c", e=2)[:, par, 4 * q:4 * q + 4], src, float(DK) ** -0.5
            return vo_hi[:, par, 512 * q:512 * q + 512].rearrange("p (j c) -> p j c", j=4), src, 1.0

        def product_lo_part(n):
            what, par, q = n // 4, n % 2, n // 2 % 2
            if what == 0:
                return a_lo[:].rearrange("p (j e) c -> p e j c", e=2)[:, par, 4 * q:4 * q + 4]
            return vo_lo[:, par, 512 * q:512 * q + 512].rearrange("p (j c) -> p j c", j=4)

        def on(turn):
            return stages(turn) if isinstance(turn, int) else ALL

        tile_x = x.rearrange("(t r h) s c -> t (h s) r c", r=NR, h=2)
        tile_out = out.rearrange("(t r h) s c -> t (h s) r c", r=NR, h=2)

        def at(ap, t):
            return ap[bass.ds(t, 1)][0]

        block = ctx.enter_context(nc.Block())

        @block.sync
        def _(sp):
            for dst, src in ((const[:], consts), (w_attn_sb[:], w_attn), (wq_ld, wq_t), (wk_ld, wk_t), (wv_ld, wv_t),
                             (wo_ld.rearrange("p (j c) -> p j c", j=J), wo.rearrange("(j p) c -> p j c", p=P)),
                             (router_sb[:], router_t),
                             (bo_sb[:], b_o.partition_broadcast(P)), (rb_sb[:], router_b.partition_broadcast(P))):
                sp.dma_start(dst, src).then_inc(w_in, 16)
            sp.wait_ge(zeroed, 1)
            for g in range(4):
                sp.dma_start(w_proj_sb[32 * g:32 * g + 16], w_proj.rearrange("(a g c) n -> g c a n", a=2, g=4)[g]).then_inc(w_in, 16)
            sp.dma_start(ex_ld.rearrange("p (e n) -> p e n", e=E), expert_w.rearrange("e p n -> p e n")).then_inc(expert_in, 16)

            def load(dst, src, arrived, tile):
                sp.dma_start(dst[:], at(src, tile)).then_inc(arrived, 16)

            load(xT, x_t, xT_in, 0)
            load(cT, ctx_t, cT_in, 0)
            load(x_sb, tile_x, x_in, 0)

            def body(i):
                u, t = i + 2, i + 1

                def context():
                    if not isinstance(i, int) or t + 1 < NT:
                        sp.wait_ge(cT_split, t + 1)
                        load(cT, ctx_t, cT_in, t + 1)

                def x_rows():
                    if not isinstance(i, int) or t + 1 < NT:
                        wait_emptied(sp, i, "PR")
                        load(x_sb, tile_x, x_in, t + 1)

                def x_columns():
                    if not isinstance(i, int) or u + 1 < NT:
                        wait_full(sp, i, "V")
                        load(xT, x_t, xT_in, u + 1)

                def place(r):
                    last_part = last_of(ACT_ORDER, [f"VB{n}" for n in range(4 * r, 4 * r + 4)])
                    moved = earlier(i, last_part) + 1
                    if not isinstance(i, int):
                        moved = sp.to_reg(moved)
                    if "l2" in on(i):
                        wait_full(sp, i, "AC1")
                    sp.wait_ge(emptied[BANK[last_part]], moved)
                    for half in range(2):
                        for par in range(2):
                            sp.dma_start(vb[64 * par:64 * par + 64, 2 * r + half], vb_raw[64 * half:64 * half + 64, r, par]).then_inc(vb_in[r], 16)

                def store():
                    sp.wait_ge(x3_ready, NR * (i - 1))
                    sp.dma_start(at(tile_out, i - 2), x3[:]).then_inc(out_done, 16)

                run(i, SP_ORDER, {"context": ("l1", context), "x_rows": ("l1", x_rows), "x_columns": ("s1", x_columns),
                                  "place": ("l1", place), "store": ("out", store)})

            turns(sp, body)
            sp.wait_ge(out_done, 16 * NT)

        @block.tensor
        def _(pe):
            def mm(o, l, r, start=True, stop=True):
                return pe.matmul(o, l, r, start=start, stop=stop)

            def mm3(o, l_hi, l_lo, r_hi, r_lo):
                mm(o, l_hi, r_hi, True, False)
                mm(o, l_hi, r_lo, False, False)
                return mm(o, l_lo, r_hi, False, True)

            pe.wait_ge(w_in, 16 * 13)
            for n in range(N_SETUP):
                what, par, q = n // 4, n % 2, n // 2 % 2
                rows = slice(64 * par, 64 * par + 64)
                left_w, right_w = ((wk_ld, wq_ld), (wv_ld, wo_ld))[what]
                if n >= 2:
                    pe.wait_ge(product_read, n - 1)
                for k in range(4):
                    j = 4 * q + k
                    cols = slice(C * j, C * j + C)
                    last = mm(ps[("B0", "B1")[par]][:, C * k:C * k + C], left_w[rows, cols], right_w[rows, cols])
                last.then_inc(product_ready, 1)
            pe.wait_ge(product_read, N_SETUP)
            pe.wait_ge(weights_split, 2)

            def body(i):
                u, t, f = i + 2, i + 1, i - 1

                def q():
                    pe.wait_ge(xT_split, u + 1)
                    return mm3(ps[BANK["Q"]][:, 0:TOK], w_qk_hi[:, 0:C], w_qk_lo[:, 0:C], xT_hi[:], xT_lo[:])

                def k():
                    pe.wait_ge(xT_split, u + 1)
                    return mm3(ps[BANK["K"]][:, 0:TOK], w_qk_hi[:, C:2 * C], w_qk_lo[:, C:2 * C], xT_hi[:], xT_lo[:])

                def v():
                    pe.wait_ge(xT_in, 16 * (u + 1))
                    for b in range(NB):
                        last = mm(ps[BANK["V"]][:, C * b:C * b + C], xT[:, b].rearrange("p a t -> p (a t)"), w_attn_sb[:, 2 * C:3 * C])
                    return last

                def s1(b):
                    wait_emptied(pe, i, "Q")
                    wait_emptied(pe, i, "K")
                    return mm(ps[BANK[f"S1_{b}"]][:], kp[:, b].rearrange("p a t -> p (a t)"), qm[:, b].rearrange("p j t -> p (j t)"))

                def y():
                    wait_emptied(pe, i - 1, "V")
                    pe.wait_ge(p1_ready, NB * (t + 1))
                    out_y = ps[BANK["Y"]][:].rearrange("p (a n) -> p a n", a=2)
                    for b in range(NB):
                        for j in range(J):
                            a, g = j // 4, j % 4
                            last = mm(out_y[32 * g:32 * g + 32, a, T * b:T * b + T], vp[:, b, j], p1[:, b, T * j:T * j + T])
                    return last

                def pr():
                    wait_emptied(pe, i, "Y")
                    for r in range(NR):
                        for a in range(2):
                            last = mm(ps[BANK["PR"]][:, C * r:C * r + C], yT[:, a, P * r:P * r + P], w_proj_sb[:, a], a == 0, a == 1)
                    return last

                def x1_turn():
                    pe.wait_ge(x1_ready, NR * (t + 1))
                    for r in range(NR):
                        last = pe.transpose(ps[BANK["X1T"]][:, P * r:P * r + P], x1[:, r], ident)
                    return last

                def z_heads(n):
                    pe.wait_ge(cT_split, t + 1)
                    for k in range(2):
                        last = mm3(ps[BANK[f"Z{n}"]][:, TOK * k:TOK * k + TOK], a_hi[:, 2 * n + k], a_lo[:, 2 * n + k], cT_hi[:], cT_lo[:])
                    return last

                def vb_part(n):
                    pe.wait_ge(cT_split, t + 1)
                    r, par, q = n // 4, n // 2 % 2, n % 2
                    cols, rows = slice(512 * q, 512 * q + 512), slice(P * r, P * r + P)
                    return mm3(ps[BANK[f"VB{n}"]][:], cT_hi[:, rows], cT_lo[:, rows], vo_hi[:, par, cols], vo_lo[:, par, cols])

                def s2(r):
                    wait_emptied(pe, i - 1, "X1T")
                    wait_emptied(pe, i - 1, last_of(ACT_ORDER, [f"Z{n}" for n in range(8)]))
                    for q in range(2):
                        for h in range(2):
                            b = 2 * r + h
                            last = mm(ps["S"][64 * h:64 * h + 64, 512 * q:512 * q + 512], x1T[:, T * b:T * b + T],
                                      z[:, b, 8 * q:8 * q + 8].rearrange("p h t -> p (h t)"))
                    return last

                def p2_turn(r, q):
                    pe.wait_ge(p2_ready, NR * i + r + 1)
                    for k in range(4):
                        j = 4 * q + k
                        last = pe.transpose(ps[BANK[f"PT{r}" + "ab"[q]]][:, P * k:P * k + P], p2[:, r, P * j:P * j + P], ident)
                    return last

                def ac(r):
                    pe.wait_ge(vb_in[r], 64 * (i + 1))
                    wait_emptied(pe, i, f"PT{r}a")
                    wait_emptied(pe, i, f"PT{r}b")
                    for j in range(J):
                        for h in range(2):
                            last = mm(ps[BANK["AC1"]][64 * h:64 * h + 64, C * r:C * r + C], p2T[:, r, j, T * h:T * h + T],
                                      vb[:, 2 * r + h, C * j:C * j + C], j == 0, j == J - 1)
                    return last

                def x2_turn():
                    pe.wait_ge(x2_ready, NR * (i + 1))
                    for r in range(NR):
                        last = pe.transpose(ps[BANK["X2T"]][:, P * r:P * r + P], x2[:, r], ident)
                    return last

                def lg():
                    wait_emptied(pe, i, "X2T")
                    for r in range(NR):
                        last = mm(ps[BANK["LG"]][:, E * r:E * r + E], x2T[:, P * r:P * r + P], router_sb[:])
                    return last

                def ff(n):
                    pe.wait_ge(x2T_split, f + 1)
                    r, q = n // 4, n % 4
                    rows, cols = slice(P * r, P * r + P), slice(512 * q, 512 * q + 512)
                    return mm3(ps[BANK[f"FF{n}"]][:], x2T_hi[:, rows], x2T_lo[:, rows], ex_hi[:, cols], ex_lo[:, cols])

                work = {"Q": q, "K": k, "V": v, "Y": y, "PR": pr, "X1T": x1_turn, "X2T": x2_turn, "LG": lg,
                        "S2_0": lambda: s2(0), "S2_1": lambda: s2(1), "AC0": lambda: ac(0), "AC1": lambda: ac(1),
                        "PT0a": lambda: p2_turn(0, 0), "PT0b": lambda: p2_turn(0, 1),
                        "PT1a": lambda: p2_turn(1, 0), "PT1b": lambda: p2_turn(1, 1)}
                for job, bank, stage in JOBS:
                    if stage not in on(i):
                        continue
                    if job == "AC0":
                        wait(pe, emptied[BANK["AC1"]], earlier(i, "AC1"))
                    elif job != "AC1":
                        wait(pe, emptied[bank], earlier(i, job))
                    if job in work:
                        last = work[job]()
                    elif job[0] == "Z":
                        last = z_heads(int(job[1:]))
                    elif job[:2] == "VB":
                        last = vb_part(int(job[2:]))
                    elif job[:2] == "S1":
                        last = s1(int(job[3:]))
                    else:
                        last = ff(int(job[2:]))
                    if bank:
                        last.then_inc(full[bank], 1)

            turns(pe, body)

        @block.scalar
        def _(act):
            def copy(dst, src, scale=1.0):
                return nc.scalar.activation(dst, src, ACT.Copy, scale=scale)

            act.wait_ge(w_in, 16 * 13)
            copy(w_qk_hi[:], w_attn_sb[:, 0:2 * C]).then_inc(weights_hi, 1)
            for n in range(N_SETUP):
                act.wait_ge(product_ready, n + 1)
                copy(*product_hi_part(n)).then_inc(product_hi, 1)
            act.wait_ge(expert_in, 16)
            copy(ex_hi[:], ex_ld).then_inc(weights_hi, 1)

            def body(i):
                u, t, f = i + 2, i + 1, i - 1

                def exp(r):
                    wait_emptied(act, i, f"S2_{r}")
                    nc.scalar.activation(p2[:, r], p2[:, r], ACT.Exp).then_inc(exp_ready, 1)

                def relu_of(b):
                    wait_full(act, i, f"S1_{b}")
                    if b >= 2:
                        wait_emptied(act, i, f"S1_{b - 2}")
                    elif not (isinstance(i, int) and u == 0):
                        wait_emptied(act, i - 1, f"S1_{b + 2}")
                    nc.scalar.activation(relu[:, b % 2], ps[BANK[f"S1_{b}"]][:], ACT.Relu).then_inc(relu_ready, 1)

                def square(b):
                    act.wait_ge(relu_ready, NB * u + b + 1)
                    nc.scalar.activation(relu[:, b % 2], relu[:, b % 2], ACT.Square).then_inc(square_ready, 1)

                def move(job, dst, src, scale=1.0):
                    wait_full(act, i, job)
                    copy(dst, src, scale).then_inc(emptied[BANK[job]], 1)

                def move_y():
                    move("Y", yT[:].rearrange("p a n -> p (a n)"), ps[BANK["Y"]][:], 1e-3)

                def move_x1T():
                    move("X1T", x1T[:], ps[BANK["X1T"]][:, 0:TOK])

                def move_x2T():
                    move("X2T", x2T[:], ps[BANK["X2T"]][:, 0:TOK])

                def move_z(n):
                    bank = ps[BANK[f"Z{n}"]][:].rearrange("p (h b t) -> p h b t", h=2, b=NB)
                    move(f"Z{n}", z[:, :, 2 * n:2 * n + 2].rearrange("p b h t -> p h b t"), bank)

                def move_p2T(r, part):
                    job, q = f"PT{r}{part}", "ab".index(part)
                    move(job, p2T[:, r, 4 * q:4 * q + 4].rearrange("p j n -> p (j n)"), ps[BANK[job]][:])

                def move_vb(n):
                    r, par, q = n // 4, n // 2 % 2, n % 2
                    if f"VB{n}" == first_of(ACT_ORDER, [f"VB{k}" for k in range(4 * r, 4 * r + 4)]):
                        if not (isinstance(i, int) and t == 0):
                            act.wait_ge(vb_in[r], 64 * t)
                    move(f"VB{n}", vb_raw[:, r, par, 512 * q:512 * q + 512], ps[BANK[f"VB{n}"]][:])

                def move_keys():
                    wait_full(act, i, "K")
                    keys = ps[BANK["K"]][:, 0:TOK].rearrange("p (b t) -> p b t", b=NB)
                    copy(kp[:, :, 0], keys, kmask[:, 0:1])
                    copy(kp[:, :, 1], keys, kmask[:, 1:2]).then_inc(emptied[BANK["K"]], 1)

                def move_values():
                    wait_full(act, i, "V")
                    values = ps[BANK["V"]][:].rearrange("p (b j c) -> p b j c", b=NB, j=J)
                    copy(vp[0:64, :, :, 0:HD], values[0:64, :, :, 0:HD])
                    copy(vp[64:128, :, :, HD:2 * HD], values[64:128, :, :, HD:2 * HD]).then_inc(emptied[BANK["V"]], 1)

                def experts_base():
                    act.wait_ge(gate_steps, GATE_STEPS * f + GEPS_STEP + 1)
                    wait(act, add_steps, ADD_STEPS * f)
                    for r in range(NR):
                        nc.scalar.activation(base3[:, r], x2[:, r], ACT.Identity, bias=geps[:, r:r + 1]).then_inc(base3_ready, 1)

                def logit_exp():
                    act.wait_ge(gate_steps, GATE_STEPS * i + 2)
                    nc.scalar.activation(logit[:], logit[:], ACT.Exp).then_inc(logit_exp_ready, 1)

                run(i, ACT_ORDER, {"exp": ("l2", exp), "VB": ("l1", move_vb), "Y": ("l1", move_y), "Z": ("l1", move_z),
                                   "X1T": ("l1", move_x1T), "K": ("s1", move_keys), "V": ("s1", move_values),
                                   "PT": ("l2", lambda rq: move_p2T(int(rq[0]), rq[1])), "relu": ("s1", relu_of), "square": ("s1", square),
                                   "X2T": ("l2", move_x2T), "base3": ("ff", experts_base), "logit_exp": ("l2", logit_exp)})

            turns(act, body)

        @block.vector
        def _(dve):
            V = nc.vector
            V.memset(w_proj_sb[:], 0.0).then_inc(zeroed, 1)
            V.memset(vp[:], 0.0)
            V.memset(prob[:], -1.0).then_inc(zeroed, 1)
            dve.wait_ge(zeroed, 2)
            dve.wait_ge(w_in, 16 * 13)
            dve.wait_ge(weights_hi, 1)
            V.tensor_tensor(w_qk_lo[:], w_attn_sb[:, 0:2 * C], w_qk_hi[:].bitcast(F32), ALU.subtract).then_inc(weights_split, 1)
            for n in range(N_SETUP):
                dve.wait_ge(product_hi, n + 1)
                hi, src, scale = product_hi_part(n)
                V.scalar_tensor_tensor(product_lo_part(n), src, scale, hi.bitcast(F32), ALU.mult, ALU.subtract).then_inc(product_read, 1)
            dve.wait_ge(weights_hi, 2)
            V.tensor_tensor(ex_lo[:], ex_ld, ex_hi[:].bitcast(F32), ALU.subtract).then_inc(weights_split, 1)

            def body(i):
                u, t, f = i + 2, i + 1, i - 1

                def hold_wait(k):
                    V.memset(scratch[:, k:k + 1], 0.0)

                norms = {1: (t, r1, x1, x1_ready), 2: (i, r2, x2, x2_ready), 3: (i - 2, r3, x3, x3_ready)}

                def stats_of(n):
                    tile, src, _, _ = norms[n]
                    if n == 1:
                        wait_emptied(dve, i, "PR")
                    elif n == 2:
                        wait_emptied(dve, i, "AC1")
                    else:
                        dve.wait_ge(add_steps, ADD_STEPS * f)
                    for r in range(NR):
                        V.bn_stats(stats[:, n - 1, r], src[:, r]).then_inc(ln_stats[n - 1], 1)

                def var(n):
                    dve.wait_ge(ln_stats[n - 1], NR * (norms[n][0] + 1))
                    hold_wait(n)
                    for r in range(NR):
                        V.bn_aggr(mv[:, n - 1, r], stats[:, n - 1, r]).then_inc(ln_var[n - 1], 1)

                def var_eps(n):
                    dve.wait_ge(ln_var[n - 1], NR * (norms[n][0] + 1))
                    V.tensor_scalar(rstd[:, n - 1], mv[:, n - 1, :, 1], LN_EPS, None, ALU.add).then_inc(ln_eps[n - 1], 1)

                def norm(n):
                    tile, src, dst, done = norms[n]
                    if n == 1:
                        wait(dve, x1b_ready, t)
                    elif n == 2:
                        wait(dve, base3_ready, NR * i)
                    else:
                        wait(dve, out_done, 16 * (i - 2))
                    dve.wait_ge(ln_rstd[n - 1], tile + 1)
                    for r in range(NR):
                        V.tensor_scalar(dst[:, r], src[:, r], mv[:, n - 1, r, 0:1], rstd[:, n - 1, r:r + 1], ALU.subtract, ALU.mult).then_inc(done, 1)

                def row_max(r):
                    wait_full(dve, i, f"S2_{r}")
                    V.tensor_reduce(rowmax[:, r], ps["S"][:].rearrange("p (h k) -> p h k", h=H), AX.X, ALU.max).then_inc(rowmax_ready, 1)

                def less_max(r):
                    dve.wait_ge(rowmax_ready, NR * i + r + 1)
                    V.tensor_tensor(p2[:, r].rearrange("p (h k) -> p h k", h=H), ps["S"][:].rearrange("p (h k) -> p h k", h=H),
                                    rowmax[:, r].unsqueeze(2).broadcast_to([P, H, T]), ALU.subtract).then_inc(emptied["S"], 1)

                def row_sum(r):
                    dve.wait_ge(exp_ready, NR * i + r + 1)
                    V.tensor_reduce(rowsum[:, r], p2[:, r].rearrange("p (h k) -> p h k", h=H), AX.X, ALU.add).then_inc(rowsum_ready, 1)

                def row_inv(r):
                    dve.wait_ge(rowsum_ready, NR * i + r + 1)
                    V.reciprocal(rowinv[:, r], rowsum[:, r]).then_inc(rowinv_ready, 1)

                def allow(b):
                    wait(dve, p1_ready, NB * u + b)
                    dve.wait_ge(relu_ready, NB * u + b + 1)
                    V.scalar_tensor_tensor(allowed[:].rearrange("p (j n) -> p j n", j=J), ps[BANK[f"S1_{b}"]][:].rearrange("p (j n) -> p j n", j=J), -100.0,
                                           causal.unsqueeze(1).broadcast_to([P, J, T]), ALU.is_ge, ALU.mult).then_inc(allowed_ready, 1)

                def pieces(b):
                    dve.wait_ge(square_ready, NB * u + b + 1)
                    V.scalar_tensor_tensor(poly[:], ps[BANK[f"S1_{b}"]][:], -0.01, relu[:, b % 2], ALU.mult, ALU.max).then_inc(emptied[BANK[f"S1_{b}"]], 1)

                def p1_of(b):
                    dve.wait_ge(allowed_ready, NB * u + b + 1)
                    wait_emptied(dve, i, f"S1_{b}")
                    V.scalar_tensor_tensor(p1[:, b], poly[:], 1.0, allowed[:], ALU.add, ALU.mult).then_inc(p1_ready, 1)

                def weigh(n):
                    r, q = n // 4, n % 4
                    job = f"FF{n}"
                    wait_full(dve, i, job)
                    if f"weigh{n}" == first_of(DVE_ORDER, [f"weigh{k}" for k in range(8)]):
                        dve.wait_ge(gate_steps, GATE_STEPS * (f + 1))
                    if f"weigh{n}" == first_of(DVE_ORDER, [f"weigh{k}" for k in range(4 * r, 4 * r + 4)]):
                        if not (isinstance(i, int) and f == 0):
                            dve.wait_ge(add_steps, ADD_STEPS * f - 5 * (NR - 1 - r))
                    V.tensor_tensor(weighted[:, r, 512 * q:512 * q + 512].rearrange("p (e c) -> p e c", e=4),
                                    ps[BANK[job]][:].rearrange("p (e c) -> p e c", e=4),
                                    gate[:, r, 4 * q:4 * q + 4].unsqueeze(2).broadcast_to([P, 4, C]), ALU.mult).then_inc(emptied[BANK[job]], 1)

                def gate_of(k):
                    if k:
                        dve.wait_ge(gate_steps, GATE_STEPS * (i if k < 2 else f) + k)
                    gate_step(k).then_inc(gate_steps, 1)

                def by_row(a, n=E):
                    return a[:].unsqueeze(2).broadcast_to([P, NR, n])

                def gate_step(k):
                    if k == 0:
                        wait_emptied(dve, i, "LG")
                        return V.tensor_reduce(lmax[:], logit[:], AX.X, ALU.max)
                    if k == 1:
                        return V.tensor_tensor(logit[:], logit[:], by_row(lmax), ALU.subtract)
                    if k == 2:
                        dve.wait_ge(logit_exp_ready, f + 1)
                        return V.tensor_reduce(lsum[:], logit[:], AX.X, ALU.add)
                    if k == 3:
                        return V.reciprocal(linv[:], lsum[:])
                    if k == 4:
                        return V.tensor_tensor(prob[:, :, 0:E], logit[:], by_row(linv), ALU.mult)
                    if k in (5, 6):
                        hold_wait(k)
                        return V.max(best[:, k - 5], prob[:, k - 5, 0:E])
                    if k == 7:
                        return V.tensor_reduce(tsum[:], best[:, :, 0:TOP], AX.X, ALU.add)
                    if k == 8:
                        return V.memset(best[:, :, TOP:8], -1.0)
                    if k in (9, 10):
                        hold_wait(k)
                        return V.match_replace(left[:, k - 9], best[:, k - 9], prob[:, k - 9], 0.0)
                    if k == 11:
                        return V.tensor_scalar(tsum[:], tsum[:], TOP_EPS, None, ALU.add)
                    if k == 12:
                        return V.tensor_tensor(gate[:], prob[:, :, 0:E], left[:, :, 0:E], ALU.subtract)
                    if k == 13:
                        return V.reciprocal(tinv[:], tsum[:])
                    if k == 14:
                        return V.tensor_tensor(gate[:], gate[:], by_row(tinv), ALU.mult)
                    if k == 15:
                        return V.tensor_reduce(gsum[:], gate[:], AX.X, ALU.add)
                    if k == GEPS_STEP:
                        wait(dve, base3_ready, NR * f)
                        return V.tensor_scalar(geps[:], gsum[:], TOP_EPS, None, ALU.mult)
                    if k == 17:
                        return V.tensor_scalar(gsum[:], gsum[:], TOP_EPS, None, ALU.max)
                    if k == 18:
                        return V.reciprocal(ginv[:], gsum[:])
                    return V.tensor_tensor(gate[:], gate[:], by_row(ginv), ALU.mult)

                def move_logits():
                    wait_full(dve, i, "LG")
                    V.tensor_tensor(logit[:], ps[BANK["LG"]][:, 0:NR * E].rearrange("p (r e) -> p r e", r=NR),
                                    rb_sb[:].unsqueeze(1).broadcast_to([P, NR, E]), ALU.add).then_inc(emptied[BANK["LG"]], 1)

                def move_queries():
                    wait_full(dve, i, "Q")
                    V.tensor_tensor(qm[:], ps[BANK["Q"]][:, 0:TOK].rearrange("p (b t) -> p b t", b=NB).unsqueeze(2).broadcast_to([P, NB, J, T]),
                                    qmask.unsqueeze(1).unsqueeze(3).broadcast_to([P, NB, J, T]), ALU.mult).then_inc(emptied[BANK["Q"]], 1)

                def projected():
                    wait_full(dve, i, "PR")
                    dve.wait_ge(x_in, 16 * (t + 1))
                    V.tensor_tensor(r1[:].rearrange("p r c -> p (r c)"), ps[BANK["PR"]][:, 0:NR * C], x_sb[:].rearrange("p r c -> p (r c)"), ALU.add).then_inc(emptied[BANK["PR"]], 1)

                def attended():
                    wait_full(dve, i, "AC1")
                    dve.wait_ge(x1b_ready, i + 1)
                    V.tensor_tensor(r2[:].rearrange("p r c -> p (r c)"), ps[BANK["AC1"]][:, 0:NR * C], x1b[:].rearrange("p r c -> p (r c)"), ALU.add).then_inc(emptied[BANK["AC1"]], 1)

                norm_stage = {1: "l1", 2: "l2", 3: "out"}
                run(i, DVE_ORDER, {"gate": (lambda k: "l2" if k < 2 else "ff", gate_of), "row_max": ("l2", row_max), "less_max": ("l2", less_max),
                                   "row_sum": ("l2", row_sum), "row_inv": ("l2", row_inv), "projected": ("l1", projected),
                                   "stats": (norm_stage.get, stats_of), "var": (norm_stage.get, var), "eps": (norm_stage.get, var_eps),
                                   "norm": (norm_stage.get, norm), "queries": ("s1", move_queries), "allow": ("s1", allow),
                                   "pieces": ("s1", pieces), "p1_": ("s1", p1_of), "weigh": ("ff", weigh), "attended": ("l2", attended),
                                   "logits": ("l2", move_logits)})

            turns(dve, body)

        @block.gpsimd
        def _(pool):
            G = nc.gpsimd
            pe_order = [job for job, _, _ in JOBS]
            last_context_job = last_of(pe_order, [f"VB{n}" for n in range(8)] + [f"Z{n}" for n in range(8)])
            last_expert_job = last_of(pe_order, [f"FF{n}" for n in range(8)])
            weighed = [last_of(DVE_ORDER, [f"weigh{n}" for n in range(4 * r, 4 * r + 4)]).replace("weigh", "FF") for r in range(NR)]
            G.memset(one[:], 1.0)
            G.memset(power[:], -0.5).then_inc(power_set, 1)
            pool.wait_ge(power_set, 1)

            def high(hi, src, hi_ready):
                G.tensor_tensor(hi, src, one[:].unsqueeze(1).broadcast_to([P, NB, T]), ALU.mult).then_inc(hi_ready, 1)

            def low(hi, lo, src, hi_ready, done, n):
                pool.wait_ge(hi_ready, n)
                G.tensor_tensor(lo, src, hi.bitcast(F32), ALU.subtract).then_inc(done, 1)

            def columns(a):
                return a[:].rearrange("p (b t) -> p b t", b=NB)

            pool.wait_ge(xT_in, 16)
            high(columns(xT_hi), xT[:, :, 0], xT_hi_ready)
            low(columns(xT_hi), columns(xT_lo), xT[:, :, 0], xT_hi_ready, xT_split, 1)

            def body(i):
                u, t, f = i + 2, i + 1, i - 1

                def root(n):
                    pool.wait_ge(ln_eps[n - 1], {1: t, 2: i, 3: i - 2}[n] + 1)
                    G.tensor_tensor(rstd[:, n - 1], rstd[:, n - 1], power[:], ALU.pow).then_inc(ln_rstd[n - 1], 1)

                def shares(r):
                    pool.wait_ge(rowinv_ready, NR * i + r + 1)
                    weights = p2[:, r].rearrange("p (h k) -> p h k", h=H)
                    G.tensor_tensor(weights, weights, rowinv[:, r].unsqueeze(2).broadcast_to([P, H, T]), ALU.mult).then_inc(p2_ready, 1)

                def add_experts(r, k):
                    tile = f - r
                    done = ADD_STEPS * tile + 5 * r
                    if k == 0:
                        wait_emptied(pool, i - r, weighed[r])
                    else:
                        pool.wait_ge(add_steps, done + k)
                    if k < 4:
                        width = 8 >> k
                        a, b = weighted[:, r, 0:width * C], weighted[:, r, width * C:2 * width * C]
                        G.tensor_tensor(a, a, b, ALU.add).then_inc(add_steps, 1)
                    else:
                        pool.wait_ge(base3_ready, NR * tile + r + 1)
                        if r == 0:
                            wait(pool, x3_ready, NR * tile)
                        G.tensor_tensor(r3[:, r], weighted[:, r, 0:C], base3[:, r], ALU.add).then_inc(add_steps, 1)

                def context_hi():
                    pool.wait_ge(cT_in, 16 * (t + 1))
                    if not (isinstance(i, int) and t == 0):
                        wait_full(pool, i - 1, last_context_job)
                    high(columns(cT_hi), columns(cT), cT_hi_ready)

                def context_lo():
                    low(columns(cT_hi), columns(cT_lo), columns(cT), cT_hi_ready, cT_split, t + 1)

                def next_x_hi():
                    if not isinstance(i, int) or u + 1 < NT:
                        pool.wait_ge(xT_in, 16 * (u + 2))
                        wait_full(pool, i, "V")
                        high(columns(xT_hi), xT[:, :, 0], xT_hi_ready)

                def next_x_lo():
                    if not isinstance(i, int) or u + 1 < NT:
                        low(columns(xT_hi), columns(xT_lo), xT[:, :, 0], xT_hi_ready, xT_split, u + 2)

                def x2_hi():
                    wait_emptied(pool, i, "X2T")
                    if "ff" in on(i):
                        wait_full(pool, i, last_expert_job)
                    high(columns(x2T_hi), columns(x2T), x2T_hi_ready)

                def x2_lo():
                    low(columns(x2T_hi), columns(x2T_lo), columns(x2T), x2T_hi_ready, x2T_split, i + 1)

                def bias_x1():
                    pool.wait_ge(x1_ready, NR * (t + 1))
                    if "l2" in on(i):
                        wait_emptied(pool, i, "AC1")
                    G.tensor_tensor(x1b[:], x1[:], bo_sb[:].unsqueeze(1).broadcast_to([P, NR, C]), ALU.add).then_inc(x1b_ready, 1)

                run(i, POOL_ORDER, {"context_hi": ("l1", context_hi), "context_lo": ("l1", context_lo), "next_x_hi": ("s1", next_x_hi),
                                    "next_x_lo": ("s1", next_x_lo), "x2_hi": ("l2", x2_hi), "x2_lo": ("l2", x2_lo),
                                    "shares": ("l2", shares), "root": ({1: "l1", 2: "l2", 3: "out"}.get, root), "bias_x1": ("l1", bias_x1),
                                    "add": (lambda r, k: ("ff", "out")[r], add_experts)})

            turns(pool, body)


def constants():
    import numpy as np
    p = np.arange(P)
    k = np.zeros((P, K_COLS), np.float32)
    k[:, K_IDENT:K_IDENT + P] = np.eye(P)
    k[:, K_CAUSAL:K_CAUSAL + T] = (p % T)[:, None] <= np.arange(T)[None, :]
    k[:, K_QMASK:K_QMASK + J] = ((p // (2 * HD))[:, None] == np.arange(J)[None, :]) * np.float32(HD ** -0.5)
    k[:, K_KMASK:K_KMASK + 2] = (p // HD % 2)[:, None] == np.arange(2)[None, :]
    return k


def kernel(x, ctx_1024, L0_attn_W_attn, L0_attn_W_proj, L0_xattn_WQ, L0_xattn_WK, L0_xattn_WV, L0_xattn_WO,
           L0_xattn_bO, L0_ffn_router_w, L0_ffn_router_b, L0_ffn_expert_w):
    import numpy as np
    import concourse.bacc as bacc
    from concourse.bass_utils import run_bass_kernel_spmd

    def columns(a):
        return np.asarray(a).reshape(NT, TOK, C).transpose(0, 2, 1)

    def by_pair(w):
        return np.asarray(w).T.reshape(J, P, C).transpose(1, 0, 2).reshape(P, J * C)

    twice = np.repeat(columns(x).reshape(NT, C, NB, 1, T), 2, axis=3)
    arrays = {
        "x": x, "x_t": twice, "ctx_t": columns(ctx_1024), "w_attn": L0_attn_W_attn, "w_proj": L0_attn_W_proj,
        "wq_t": by_pair(L0_xattn_WQ), "wk_t": by_pair(L0_xattn_WK), "wv_t": by_pair(L0_xattn_WV), "wo": L0_xattn_WO,
        "b_o": L0_xattn_bO, "router_t": np.asarray(L0_ffn_router_w).T, "router_b": L0_ffn_router_b,
        "expert_w": L0_ffn_expert_w, "consts": constants(),
    }
    arrays = {n: np.ascontiguousarray(a) for n, a in arrays.items()}
    nc = bacc.Bacc("TRN2", target_bir_lowering=False, num_devices=1)
    args = {n: nc.dram_tensor("in_" + n, a.shape, mybir.dt.from_np(a.dtype), kind="ExternalInput").ap() for n, a in arrays.items()}
    out = nc.dram_tensor("out_0", (B, T, C), F32, kind="ExternalOutput").ap()
    decoder(nc, out=out, **args)
    r = run_bass_kernel_spmd(nc, [{"in_" + n: a for n, a in arrays.items()}], core_ids=[0])
    return r.results[0]["out_0"]
```

```python
from contextlib import ExitStack

import concourse.bass as bass
from concourse import mybir

P = 128
ALU = mybir.AluOpType
ACT = mybir.ActivationFunctionType
AX = mybir.AxisListType
F32 = mybir.dt.float32
F32R = mybir.dt.float32r

C = 128
T = 64
B = 128
H = 16
J = H // 2
E = 16
TOP = 6
NB = 4
NR = NB // 2
TOK = NB * T
NT = B // NB
HD = C // H
DK = 64
LN_EPS = 1e-5
TOP_EPS = 1e-10
GATE_STEPS = 20
GEPS_STEP = 16
ADD_STEPS = 10

K_IDENT = 0
K_CAUSAL = K_IDENT + P
K_QMASK = K_CAUSAL + T
K_KMASK = K_QMASK + J
K_COLS = K_KMASK + 2

JOBS = [
    ("S2_0", "S", "l2"), ("Q", "B0", "s1"), ("K", "B4", "s1"), ("Y", "B1", "l1"), ("VB0", "B0", "l1"),
    ("V", "B2", "s1"), ("VB1", "B3", "l1"), ("VB3", "B4", "l1"), ("S2_1", "S", "l2"), ("VB4", "B0", "l1"),
    ("S1_0", "B1", "s1"), ("Z7", "B3", "l1"), ("PR", "B4", "l1"), ("Z1", "B5", "l1"), ("Z5", "B2", "l1"),
    ("FF0", "B3", "ff"), ("VB2", "B0", "l1"), ("S1_1", "B4", "s1"), ("product0", "B5", "setup"),
    ("PT0a", "B5", "l2"), ("PT0b", "B1", "l2"), ("Z2", "B2", "l1"), ("VB7", "B0", "l1"), ("FF1", "B5", "ff"),
    ("AC0", "", "l2"), ("PT1b", "B2", "l2"), ("PT1a", "B0", "l2"), ("FF2", "B4", "ff"), ("FF3", "B2", "ff"),
    ("Z4", "B5", "l1"), ("product1", "B2", "setup"), ("S1_2", "B3", "s1"), ("AC1", "B1", "l2"),
    ("Z0", "B4", "l1"), ("Z3", "B2", "l1"), ("FF6", "B0", "ff"), ("product2", "B0", "setup"),
    ("product3", "B5", "setup"), ("Z6", "B1", "l1"), ("FF7", "B2", "ff"), ("product4", "B2", "setup"),
    ("S1_3", "B0", "s1"), ("product5", "B4", "setup"), ("X1T", "B5", "l1"), ("FF4", "B4", "ff"),
    ("VB6", "B3", "l1"), ("X2T", "B1", "l2"), ("product6", "B2", "setup"), ("FF5", "B5", "ff"),
    ("product7", "B3", "setup"), ("VB5", "B2", "l1"), ("LG", "B1", "l2"),
]
BANK = {job: bank for job, bank, _ in JOBS}
BANKS = ["B0", "B1", "B2", "B3", "B4", "B5", "S"]

SP_ORDER = """
    x_columns place0 store context x_rows place1
""".split()
ACT_ORDER = """
    Q K queries_hi0 VB0 exp0 Y queries_hi1 VB1 V VB3 product_hi0 VB4 relu0 Z7 square0 Z1 exp1 Z5 VB2 PT0a
    PT0b relu1 product_hi1 product_hi2 square1 Z2 VB7 PT1b product_hi3 PT1a Z4 relu2 square2 product_hi4 Z3
    Z0 base3 Z6 X1T relu3 product_hi5 X2T square3 VB6 product_hi6 VB5 logit_exp product_hi7
""".split()
DVE_ORDER = """
    row_max0 less_max0 gate2 gate3 keys_lo0 keys_lo1 queries_lo row_sum0 gate4 row_inv0 row_max1 gate5
    less_max1 allow0 gate6 projected gate7 gate8 pieces0 product_lo0 product_lo1 stats1 gate9 gate10
    row_sum1 p1_0 row_inv1 product_lo2 gate11 gate12 var1 allow1 pieces1 gate13 gate14 gate15 eps1 gate16
    gate17 gate18 gate19 weigh1 product_lo3 weigh0 weigh3 p1_1 weigh2 stats3 var3 norm1 allow2 product_lo4
    attended stats2 eps3 var2 eps2 weigh6 pieces2 norm2 weigh7 norm3 p1_2 product_lo5 weigh4 allow3 pieces3
    logits gate0 p1_3 product_lo6 product_lo7 gate1 weigh5
""".split()
POOL_ORDER = """
    context_hi context_lo q_hi q_lo add1.0 shares0 add1.1 add1.2 experts_hi next_x_hi shares1 next_x_lo
    add1.3 root1 add1.4 add0.0 root2 experts_lo root3 add0.1 bias_x1 add0.2 x2_hi add0.3 x2_lo add0.4
""".split()


def first_of(order, steps):
    return min(steps, key=order.index)


def last_of(order, steps):
    return max(steps, key=order.index)


def stages(turn):
    return ({"setup"} if turn == -2 else set()) | {s for s, t in (("s1", turn + 2), ("l1", turn + 1), ("l2", turn), ("ff", turn - 1), ("out", turn - 2)) if 0 <= t < NT}


def fills(bank, on, before=None):
    n = 0
    for job, b, stage in JOBS:
        if job == before:
            break
        n += b == bank and stage in on
    return n


ALL = {"s1", "l1", "l2", "ff", "out"}


def earlier(turn, job):
    bank = BANK[job]
    first = sum(fills(bank, stages(u)) for u in range(-2, 1))
    if isinstance(turn, int) and not 1 <= turn <= NT - 3:
        return sum(fills(bank, stages(u)) for u in range(-2, turn)) + fills(bank, stages(turn), job)
    return (turn - 1) * fills(bank, ALL) + (first + fills(bank, ALL, job))


def decoder(nc, x, x_t, ctx_t, w_attn, w_proj, wq_t, wk_t, wv_t, wo, b_o, router_t, router_b, expert_w, consts, out):
    ctx = ExitStack()
    with ctx:
        def sb(name, shape, dt=F32):
            return ctx.enter_context(nc.sbuf_tensor(name, shape, dt))

        def sem(name):
            return ctx.enter_context(nc.semaphore(name))

        ps = {}
        for b in BANKS:
            ps[b] = ctx.enter_context(nc.psum_tensor("ps_" + b, [P, 1024 if b == "S" else 512], F32))
        full = {b: sem("full_" + b) for b in BANKS}
        emptied = {b: sem("emptied_" + b) for b in BANKS}

        const = sb("const", [P, K_COLS])
        ident = const[:, K_IDENT:K_IDENT + P]
        causal = const[:, K_CAUSAL:K_CAUSAL + T]
        qmask = const[:, K_QMASK:K_QMASK + J]
        kmask = const[:, K_KMASK:K_KMASK + 2]
        w_attn_sb = sb("w_attn_sb", [P, 3 * C])
        w_proj_sb = sb("w_proj_sb", [P, C])
        w_qk_hi, w_qk_lo = sb("w_qk_hi", [P, 2 * C], F32R), sb("w_qk_lo", [P, 2 * C], F32R)
        bo_sb = sb("bo_sb", [P, C])
        rb_sb = sb("rb_sb", [P, E])
        router_sb = sb("router_sb", [P, E])
        a_hi, a_lo = sb("a_hi", [P, H, C], F32R), sb("a_lo", [P, H, C], F32R)
        vo_hi, vo_lo = sb("vo_hi", [P, 2, J * C], F32R), sb("vo_lo", [P, 2, J * C], F32R)
        ex_hi, ex_lo = sb("ex_hi", [P, E * C], F32R), sb("ex_lo", [P, E * C], F32R)

        x_sb = sb("x_sb", [P, NR, C])
        xT = sb("xT", [P, NB, 2, T])
        cT = sb("cT", [P, TOK])
        xT_hi, xT_lo = sb("xT_hi", [P, TOK], F32R), sb("xT_lo", [P, TOK], F32R)
        cT_hi, cT_lo = sb("cT_hi", [P, TOK], F32R), sb("cT_lo", [P, TOK], F32R)
        q_sb = sb("q_sb", [P, TOK])
        q_hi, q_lo = sb("q_hi", [P, TOK]), sb("q_lo", [P, TOK])
        qm_hi, qm_lo = sb("qm_hi", [P, NB, J, T], F32R), sb("qm_lo", [P, NB, J, T], F32R)
        kp_hi, kp_lo = sb("kp_hi", [P, NB, 2, T], F32R), sb("kp_lo", [P, NB, 2, T], F32R)
        vp = sb("vp", [P, NB * J // 2, 4, 16])
        relu = sb("relu", [P, 2, J * T])
        allowed = sb("allowed", [P, J * T])
        poly = sb("poly", [P, J * T])
        p1 = sb("p1", [P, NB, J * T])
        yT = sb("yT", [P, TOK])
        r1 = sb("r1", [P, NR, C])
        x1 = sb("x1", [P, NR, C])
        x1b = sb("x1b", [P, NR, C])
        x1T = sb("x1T", [P, TOK])
        z = sb("z", [P, NB, H, T])
        p2 = sb("p2", [P, NR, H * T])
        p2T = sb("p2T", [P, NR, J, P])
        vb_raw = sb("vb_raw", [P, NR, 2, J * C])
        vb = sb("vb", [P, NB, J * C])
        r2 = sb("r2", [P, NR, C])
        x2 = sb("x2", [P, NR, C])
        x2T = sb("x2T", [P, TOK])
        x2T_hi, x2T_lo = sb("x2T_hi", [P, TOK], F32R), sb("x2T_lo", [P, TOK], F32R)
        weighted = sb("weighted", [P, NR, E * C])
        base3, r3 = sb("base3", [P, NR, C]), sb("r3", [P, NR, C])
        x3 = sb("x3", [P, NR, C])
        rowmax, rowsum, rowinv = sb("rowmax", [P, NR, H]), sb("rowsum", [P, NR, H]), sb("rowinv", [P, NR, H])
        stats, mv, rstd = sb("stats", [P, 3, NR, 6]), sb("mv", [P, 3, NR, 2]), sb("rstd", [P, 3, NR])
        power, one, scratch = sb("power", [P, NR]), sb("one", [P, 1]), sb("scratch", [P, GATE_STEPS])
        logit = sb("logit", [P, NR, E])
        lmax, lsum, linv = sb("lmax", [P, NR]), sb("lsum", [P, NR]), sb("linv", [P, NR])
        prob, left = sb("prob", [P, NR, E + 2]), sb("left", [P, NR, E + 2])
        best = sb("best", [P, NR, 8])
        gate = sb("gate", [P, NR, E])
        tsum, tinv = sb("tsum", [P, NR]), sb("tinv", [P, NR])
        gsum, ginv, geps = sb("gsum", [P, NR]), sb("ginv", [P, NR]), sb("geps", [P, NR])

        wq_ld, wk_ld = weighted[:, 0, 0:J * C], weighted[:, 0, J * C:2 * J * C]
        wv_ld, wo_ld = weighted[:, 1, 0:J * C], weighted[:, 1, J * C:2 * J * C]
        ex_ld = p2T[:].rearrange("p r j n -> p (r j n)")

        attn_in, w_in, expert_in = sem("attn_in"), sem("w_in"), sem("expert_in")
        zeroed, power_set = sem("zeroed"), sem("power_set")
        product_hi_ready = sem("product_hi_ready")
        attn_hi, attn_split, expert_hi, expert_split = sem("attn_hi"), sem("attn_split"), sem("expert_hi"), sem("expert_split")
        x_in, xT_in, cT_in = sem("x_in"), sem("xT_in"), sem("cT_in")
        xT_hi_ready, xT_split = sem("xT_hi_ready"), sem("xT_split")
        cT_hi_ready, cT_split = sem("cT_hi_ready"), sem("cT_split")
        q_hi_ready, q_lo_ready, k_hi_ready, k_lo_ready, qm_hi_ready, qm_lo_ready = (sem(n) for n in (
            "q_hi_ready", "q_lo_ready", "k_hi_ready", "k_lo_ready", "qm_hi_ready", "qm_lo_ready"))
        relu_ready, square_ready, allowed_ready, p1_ready = sem("relu_ready"), sem("square_ready"), sem("allowed_ready"), sem("p1_ready")
        x1_ready, x1b_ready = sem("x1_ready"), sem("x1b_ready")
        vb_in = [sem(f"vb_in{r}") for r in range(NR)]
        rowmax_ready, exp_ready, rowsum_ready, rowinv_ready, p2_ready = sem("rowmax_ready"), sem("exp_ready"), sem("rowsum_ready"), sem("rowinv_ready"), sem("p2_ready")
        x2_ready, x2T_hi_ready, x2T_split = sem("x2_ready"), sem("x2T_hi_ready"), sem("x2T_split")
        logit_exp_ready, gate_steps = sem("logit_exp_ready"), sem("gate_steps")
        add_steps = sem("add_steps")
        base3_ready, x3_ready, out_done = sem("base3_ready"), sem("x3_ready"), sem("out_done")
        ln_stats, ln_var, ln_eps, ln_rstd = ([sem(f"ln{n}_{what}") for n in (1, 2, 3)] for what in ("stats", "var", "eps", "rstd"))

        N_WEIGHTS = 16 * 8

        def wait(eng, s, n):
            if not (isinstance(n, int) and n == 0):
                eng.wait_ge(s, n)

        def wait_full(eng, turn, job):
            wait(eng, full[BANK[job]], earlier(turn, job) + 1)

        def wait_emptied(eng, turn, job):
            wait(eng, emptied[BANK[job]], earlier(turn, job) + 1)

        def run(turn, order, steps):
            for word in order:
                name = max((n for n in steps if word.startswith(n)), key=len)
                rest = word[len(name):]
                args = [int(a) if a.isdigit() else a for a in rest.split(".")] if rest else []
                stage, step = steps[name]
                if (stage if isinstance(stage, str) else stage(*args)) in on(turn):
                    step(*args)

        def turns(eng, body):
            for i in range(-2, 3):
                body(i)
            with eng.Fori(3, NT - 3) as i:
                body(i)
            for i in range(NT - 3, NT + 2):
                body(i)

        def product_hi_part(n):
            what, par, q = n // 4, n % 2, n // 2 % 2
            src = ps[BANK[f"product{n}"]][:].rearrange("p (j c) -> p j c", j=4)
            if what == 0:
                return a_hi[:].rearrange("p (j e) c -> p e j c", e=2)[:, par, 4 * q:4 * q + 4], src, float(DK) ** -0.5
            return vo_hi[:, par, 512 * q:512 * q + 512].rearrange("p (j c) -> p j c", j=4), src, 1.0

        def product_lo_part(n):
            what, par, q = n // 4, n % 2, n // 2 % 2
            if what == 0:
                return a_lo[:].rearrange("p (j e) c -> p e j c", e=2)[:, par, 4 * q:4 * q + 4]
            return vo_lo[:, par, 512 * q:512 * q + 512].rearrange("p (j c) -> p j c", j=4)

        def on(turn):
            return stages(turn) if isinstance(turn, int) else ALL

        tile_x = x.rearrange("(t r h) s c -> t (h s) r c", r=NR, h=2)
        tile_out = out.rearrange("(t r h) s c -> t (h s) r c", r=NR, h=2)

        def at(ap, t):
            return ap[bass.ds(t, 1)][0]

        block = ctx.enter_context(nc.Block())

        @block.sync
        def _(sp):
            def load(dst, src, arrived, tile):
                sp.dma_start(dst[:], at(src, tile)).then_inc(arrived, 16)

            for dst, src in ((const[:], consts), (w_attn_sb[:], w_attn)):
                sp.dma_start(dst, src).then_inc(attn_in, 16)
            load(xT, x_t, xT_in, 0)
            for dst, src in ((wq_ld, wq_t), (wk_ld, wk_t), (wv_ld, wv_t),
                             (wo_ld.rearrange("p (j c) -> p j c", j=J), wo.rearrange("(j p) c -> p j c", p=P)),
                             (router_sb[:], router_t), (w_proj_sb[:], w_proj),
                             (bo_sb[:], b_o.partition_broadcast(P)), (rb_sb[:], router_b.partition_broadcast(P))):
                sp.dma_start(dst, src).then_inc(w_in, 16)
            load(cT, ctx_t, cT_in, 0)
            sp.dma_start(ex_ld.rearrange("p (e n) -> p e n", e=E), expert_w.rearrange("e p n -> p e n")).then_inc(expert_in, 16)
            load(x_sb, tile_x, x_in, 0)

            def body(i):
                u, t = i + 2, i + 1

                def context():
                    if not isinstance(i, int) or t + 1 < NT:
                        sp.wait_ge(cT_split, t + 1)
                        load(cT, ctx_t, cT_in, t + 1)

                def x_rows():
                    if not isinstance(i, int) or t + 1 < NT:
                        wait_emptied(sp, i, "PR")
                        load(x_sb, tile_x, x_in, t + 1)

                def x_columns():
                    if not isinstance(i, int) or u + 1 < NT:
                        wait_full(sp, i, "V")
                        load(xT, x_t, xT_in, u + 1)

                def place(r):
                    last_part = last_of(ACT_ORDER, [f"VB{n}" for n in range(4 * r, 4 * r + 4)])
                    moved = earlier(i, last_part) + 1
                    if not isinstance(i, int):
                        moved = sp.to_reg(moved)
                    if "l2" in on(i):
                        wait_full(sp, i, "AC1")
                    sp.wait_ge(emptied[BANK[last_part]], moved)
                    for half in range(2):
                        for par in range(2):
                            sp.dma_start(vb[64 * par:64 * par + 64, 2 * r + half], vb_raw[64 * half:64 * half + 64, r, par]).then_inc(vb_in[r], 16)

                def store():
                    sp.wait_ge(x3_ready, NR * (i - 1))
                    sp.dma_start(at(tile_out, i - 2), x3[:]).then_inc(out_done, 16)

                run(i, SP_ORDER, {"context": ("l1", context), "x_rows": ("l1", x_rows), "x_columns": ("s1", x_columns),
                                  "place": ("l1", place), "store": ("out", store)})

            turns(sp, body)
            sp.wait_ge(out_done, 16 * NT)

        @block.tensor
        def _(pe):
            def mm(o, l, r, start=True, stop=True):
                return pe.matmul(o, l, r, start=start, stop=stop)

            def mm3(o, l_hi, l_lo, r_hi, r_lo):
                mm(o, l_hi, r_hi, True, False)
                mm(o, l_hi, r_lo, False, False)
                return mm(o, l_lo, r_hi, False, True)

            pe.wait_ge(attn_in, 32)
            pe.wait_ge(attn_split, 1)

            def body(i):
                u, t, f = i + 2, i + 1, i - 1

                def product(n):
                    pe.wait_ge(w_in, N_WEIGHTS)
                    what, par, q = n // 4, n % 2, n // 2 % 2
                    rows = slice(64 * par, 64 * par + 64)
                    left_w, right_w = ((wk_ld, wq_ld), (wv_ld, wo_ld))[what]
                    for k in range(4):
                        cols = slice(C * (4 * q + k), C * (4 * q + k) + C)
                        last = mm(ps[BANK[f"product{n}"]][:, C * k:C * k + C], left_w[rows, cols], right_w[rows, cols])
                    return last

                def products_moved(what):
                    if isinstance(i, int) and t == 0:
                        for n in range(4 * what, 4 * what + 4):
                            wait_emptied(pe, -2, f"product{n}")

                def q():
                    pe.wait_ge(xT_split, u + 1)
                    return mm3(ps[BANK["Q"]][:, 0:TOK], w_qk_hi[:, 0:C], w_qk_lo[:, 0:C], xT_hi[:], xT_lo[:])

                def k():
                    pe.wait_ge(xT_split, u + 1)
                    return mm3(ps[BANK["K"]][:, 0:TOK], w_qk_hi[:, C:2 * C], w_qk_lo[:, C:2 * C], xT_hi[:], xT_lo[:])

                def v():
                    pe.wait_ge(xT_in, 16 * (u + 1))
                    for b in range(NB):
                        last = mm(ps[BANK["V"]][:, C * b:C * b + C], xT[:, b].rearrange("p a t -> p (a t)"), w_attn_sb[:, 2 * C:3 * C])
                    return last

                def s1(b):
                    pe.wait_ge(qm_hi_ready, 2 * (u + 1))
                    pe.wait_ge(qm_lo_ready, u + 1)
                    wait_emptied(pe, i, "K")
                    k_hi, k_lo = (a[:, b].rearrange("p a t -> p (a t)") for a in (kp_hi, kp_lo))
                    q_hi, q_lo = (a[:, b].rearrange("p j t -> p (j t)") for a in (qm_hi, qm_lo))
                    return mm3(ps[BANK[f"S1_{b}"]][:], k_hi, k_lo, q_hi, q_lo)

                def y():
                    wait_emptied(pe, i - 1, "V")
                    pe.wait_ge(p1_ready, NB * (t + 1))
                    for b in range(NB):
                        for second in range(2):
                            for g in range(J // 2):
                                j = 2 * g + second
                                values = vp[:, J // 2 * b + g, second:second + 2].rearrange("p z c -> p (z c)")
                                last = mm(ps[BANK["Y"]][32 * g:32 * g + 32, T * b:T * b + T], values, p1[:, b, T * j:T * j + T], second == 0, second == 1)
                    return last

                def pr():
                    wait_emptied(pe, i, "Y")
                    for r in range(NR):
                        last = mm(ps[BANK["PR"]][:, C * r:C * r + C], yT[:, P * r:P * r + P], w_proj_sb[:])
                    return last

                def x1_turn():
                    pe.wait_ge(x1_ready, NR * (t + 1))
                    for r in range(NR):
                        last = pe.transpose(ps[BANK["X1T"]][:, P * r:P * r + P], x1[:, r], ident)
                    return last

                def z_heads(n):
                    products_moved(0)
                    pe.wait_ge(cT_split, t + 1)
                    for k in range(2):
                        last = mm3(ps[BANK[f"Z{n}"]][:, TOK * k:TOK * k + TOK], a_hi[:, 2 * n + k], a_lo[:, 2 * n + k], cT_hi[:], cT_lo[:])
                    return last

                def vb_part(n):
                    products_moved(1)
                    pe.wait_ge(cT_split, t + 1)
                    r, par, q = n // 4, n // 2 % 2, n % 2
                    cols, rows = slice(512 * q, 512 * q + 512), slice(P * r, P * r + P)
                    return mm3(ps[BANK[f"VB{n}"]][:], cT_hi[:, rows], cT_lo[:, rows], vo_hi[:, par, cols], vo_lo[:, par, cols])

                def s2(r):
                    wait_emptied(pe, i - 1, "X1T")
                    wait_emptied(pe, i - 1, last_of(ACT_ORDER, [f"Z{n}" for n in range(8)]))
                    for q in range(2):
                        for h in range(2):
                            b = 2 * r + h
                            last = mm(ps["S"][64 * h:64 * h + 64, 512 * q:512 * q + 512], x1T[:, T * b:T * b + T],
                                      z[:, b, 8 * q:8 * q + 8].rearrange("p h t -> p (h t)"))
                    return last

                def p2_turn(r, q):
                    pe.wait_ge(p2_ready, NR * i + r + 1)
                    for k in range(4):
                        j = 4 * q + k
                        last = pe.transpose(ps[BANK[f"PT{r}" + "ab"[q]]][:, P * k:P * k + P], p2[:, r, P * j:P * j + P], ident)
                    return last

                def ac(r):
                    pe.wait_ge(vb_in[r], 64 * (i + 1))
                    wait_emptied(pe, i, f"PT{r}a")
                    wait_emptied(pe, i, f"PT{r}b")
                    for j in range(J):
                        for h in range(2):
                            last = mm(ps[BANK["AC1"]][64 * h:64 * h + 64, C * r:C * r + C], p2T[:, r, j, T * h:T * h + T],
                                      vb[:, 2 * r + h, C * j:C * j + C], j == 0, j == J - 1)
                    return last

                def x2_turn():
                    pe.wait_ge(x2_ready, NR * (i + 1))
                    for r in range(NR):
                        last = pe.transpose(ps[BANK["X2T"]][:, P * r:P * r + P], x2[:, r], ident)
                    return last

                def lg():
                    wait_emptied(pe, i, "X2T")
                    for r in range(NR):
                        last = mm(ps[BANK["LG"]][:, E * r:E * r + E], x2T[:, P * r:P * r + P], router_sb[:])
                    return last

                def ff(n):
                    if isinstance(i, int) and f == 0:
                        pe.wait_ge(expert_split, 1)
                    pe.wait_ge(x2T_split, f + 1)
                    r, q = n // 4, n % 4
                    rows, cols = slice(P * r, P * r + P), slice(512 * q, 512 * q + 512)
                    return mm3(ps[BANK[f"FF{n}"]][:], x2T_hi[:, rows], x2T_lo[:, rows], ex_hi[:, cols], ex_lo[:, cols])

                work = {"Q": q, "K": k, "V": v, "Y": y, "PR": pr, "X1T": x1_turn, "X2T": x2_turn, "LG": lg,
                        "S2_0": lambda: s2(0), "S2_1": lambda: s2(1), "AC0": lambda: ac(0), "AC1": lambda: ac(1),
                        "PT0a": lambda: p2_turn(0, 0), "PT0b": lambda: p2_turn(0, 1),
                        "PT1a": lambda: p2_turn(1, 0), "PT1b": lambda: p2_turn(1, 1)}
                for job, bank, stage in JOBS:
                    if stage not in on(i):
                        continue
                    if job == "AC0":
                        wait(pe, emptied[BANK["AC1"]], earlier(i, "AC1"))
                    elif job != "AC1":
                        wait(pe, emptied[bank], earlier(i, job))
                    if job in work:
                        last = work[job]()
                    elif job[:7] == "product":
                        last = product(int(job[7:]))
                    elif job[0] == "Z":
                        last = z_heads(int(job[1:]))
                    elif job[:2] == "VB":
                        last = vb_part(int(job[2:]))
                    elif job[:2] == "S1":
                        last = s1(int(job[3:]))
                    else:
                        last = ff(int(job[2:]))
                    if bank:
                        last.then_inc(full[bank], 1)

            turns(pe, body)

        @block.scalar
        def _(act):
            def copy(dst, src, scale=1.0):
                return nc.scalar.activation(dst, src, ACT.Copy, scale=scale)

            act.wait_ge(attn_in, 32)
            copy(w_qk_hi[:], w_attn_sb[:, 0:2 * C]).then_inc(attn_hi, 1)
            act.wait_ge(zeroed, 1)

            def body(i):
                u, t, f = i + 2, i + 1, i - 1

                def product_hi(n):
                    wait_full(act, i, f"product{n}")
                    copy(*product_hi_part(n)).then_inc(product_hi_ready, 1)

                def exp(r):
                    wait_emptied(act, i, f"S2_{r}")
                    nc.scalar.activation(p2[:, r], p2[:, r], ACT.Exp).then_inc(exp_ready, 1)

                def relu_of(b):
                    wait_full(act, i, f"S1_{b}")
                    if b >= 2:
                        wait_emptied(act, i, f"S1_{b - 2}")
                    elif not (isinstance(i, int) and u == 0):
                        wait_emptied(act, i - 1, f"S1_{b + 2}")
                    nc.scalar.activation(relu[:, b % 2], ps[BANK[f"S1_{b}"]][:], ACT.Relu).then_inc(relu_ready, 1)

                def square(b):
                    act.wait_ge(relu_ready, NB * u + b + 1)
                    nc.scalar.activation(relu[:, b % 2], relu[:, b % 2], ACT.Square).then_inc(square_ready, 1)

                def move(job, dst, src, scale=1.0):
                    wait_full(act, i, job)
                    copy(dst, src, scale).then_inc(emptied[BANK[job]], 1)

                def move_y():
                    move("Y", yT[:], ps[BANK["Y"]][:, 0:TOK], 1e-3)

                def move_x1T():
                    move("X1T", x1T[:], ps[BANK["X1T"]][:, 0:TOK])

                def move_x2T():
                    move("X2T", x2T[:], ps[BANK["X2T"]][:, 0:TOK])

                def move_z(n):
                    bank = ps[BANK[f"Z{n}"]][:].rearrange("p (h b t) -> p h b t", h=2, b=NB)
                    move(f"Z{n}", z[:, :, 2 * n:2 * n + 2].rearrange("p b h t -> p h b t"), bank)

                def move_p2T(r, part):
                    job, q = f"PT{r}{part}", "ab".index(part)
                    move(job, p2T[:, r, 4 * q:4 * q + 4].rearrange("p j n -> p (j n)"), ps[BANK[job]][:])

                def move_vb(n):
                    r, par, q = n // 4, n // 2 % 2, n % 2
                    if f"VB{n}" == first_of(ACT_ORDER, [f"VB{k}" for k in range(4 * r, 4 * r + 4)]):
                        if not (isinstance(i, int) and t == 0):
                            act.wait_ge(vb_in[r], 64 * t)
                    move(f"VB{n}", vb_raw[:, r, par, 512 * q:512 * q + 512], ps[BANK[f"VB{n}"]][:])

                def move_keys():
                    wait_full(act, i, "K")
                    keys = ps[BANK["K"]][:, 0:TOK].rearrange("p (b t) -> p b t", b=NB)
                    copy(kp_hi[:, :, 0], keys, kmask[:, 0:1])
                    copy(kp_hi[:, :, 1], keys, kmask[:, 1:2]).then_inc(k_hi_ready, 1)

                def move_q():
                    move("Q", q_sb[:], ps[BANK["Q"]][:, 0:TOK], float(HD) ** -0.5)

                def queries_hi(half):
                    act.wait_ge(q_hi_ready, u + 1)
                    for j in range(4 * half, 4 * half + 4):
                        last = copy(qm_hi[:, :, j], q_hi[:].rearrange("p (b t) -> p b t", b=NB), qmask[:, j:j + 1])
                    last.then_inc(qm_hi_ready, 1)

                def move_values():
                    wait_full(act, i, "V")
                    values = ps[BANK["V"]][:].rearrange("p (n o c) -> p n o c", o=2, c=2 * HD)
                    places = vp[:].rearrange("p n (o z) c -> p n o z c", o=2)[:, :, :, 0]
                    copy(places[0:64, :, :, 0:HD], values[0:64, :, :, 0:HD])
                    copy(places[64:128, :, :, HD:2 * HD], values[64:128, :, :, HD:2 * HD]).then_inc(emptied[BANK["V"]], 1)

                def experts_base():
                    act.wait_ge(gate_steps, GATE_STEPS * f + GEPS_STEP + 1)
                    wait(act, add_steps, ADD_STEPS * f)
                    for r in range(NR):
                        nc.scalar.activation(base3[:, r], x2[:, r], ACT.Identity, bias=geps[:, r:r + 1]).then_inc(base3_ready, 1)

                def logit_exp():
                    act.wait_ge(gate_steps, GATE_STEPS * i + 2)
                    nc.scalar.activation(logit[:], logit[:], ACT.Exp).then_inc(logit_exp_ready, 1)

                run(i, ACT_ORDER, {"product_hi": ("setup", product_hi), "exp": ("l2", exp), "VB": ("l1", move_vb), "Y": ("l1", move_y), "Z": ("l1", move_z),
                                   "X1T": ("l1", move_x1T), "K": ("s1", move_keys), "Q": ("s1", move_q), "queries_hi": ("s1", queries_hi), "V": ("s1", move_values),
                                   "PT": ("l2", lambda rq: move_p2T(int(rq[0]), rq[1])), "relu": ("s1", relu_of), "square": ("s1", square),
                                   "X2T": ("l2", move_x2T), "base3": ("ff", experts_base), "logit_exp": ("l2", logit_exp)})

            turns(act, body)

        @block.vector
        def _(dve):
            V = nc.vector
            V.memset(vp[:], 0.0).then_inc(zeroed, 1)
            V.memset(prob[:], -1.0).then_inc(zeroed, 1)
            dve.wait_ge(zeroed, 2)
            dve.wait_ge(attn_in, 32)
            dve.wait_ge(attn_hi, 1)
            V.tensor_tensor(w_qk_lo[:], w_attn_sb[:, 0:2 * C], w_qk_hi[:].bitcast(F32), ALU.subtract).then_inc(attn_split, 1)

            def body(i):
                u, t, f = i + 2, i + 1, i - 1

                def hold_wait(k):
                    V.memset(scratch[:, k:k + 1], 0.0)

                norms = {1: (t, r1, x1, x1_ready), 2: (i, r2, x2, x2_ready), 3: (i - 2, r3, x3, x3_ready)}

                def stats_of(n):
                    tile, src, _, _ = norms[n]
                    if n == 1:
                        wait_emptied(dve, i, "PR")
                    elif n == 2:
                        wait_emptied(dve, i, "AC1")
                    else:
                        dve.wait_ge(add_steps, ADD_STEPS * f)
                    for r in range(NR):
                        V.bn_stats(stats[:, n - 1, r], src[:, r]).then_inc(ln_stats[n - 1], 1)

                def var(n):
                    dve.wait_ge(ln_stats[n - 1], NR * (norms[n][0] + 1))
                    hold_wait(n)
                    for r in range(NR):
                        V.bn_aggr(mv[:, n - 1, r], stats[:, n - 1, r]).then_inc(ln_var[n - 1], 1)

                def var_eps(n):
                    dve.wait_ge(ln_var[n - 1], NR * (norms[n][0] + 1))
                    V.tensor_scalar(rstd[:, n - 1], mv[:, n - 1, :, 1], LN_EPS, None, ALU.add).then_inc(ln_eps[n - 1], 1)

                def norm(n):
                    tile, src, dst, done = norms[n]
                    if n == 1:
                        wait(dve, x1b_ready, t)
                    elif n == 2:
                        wait(dve, base3_ready, NR * i)
                    else:
                        wait(dve, out_done, 16 * (i - 2))
                    dve.wait_ge(ln_rstd[n - 1], tile + 1)
                    for r in range(NR):
                        V.tensor_scalar(dst[:, r], src[:, r], mv[:, n - 1, r, 0:1], rstd[:, n - 1, r:r + 1], ALU.subtract, ALU.mult).then_inc(done, 1)

                def product_lo(n):
                    dve.wait_ge(w_in, N_WEIGHTS)
                    dve.wait_ge(product_hi_ready, n + 1)
                    hi, src, scale = product_hi_part(n)
                    V.scalar_tensor_tensor(product_lo_part(n), src, scale, hi.bitcast(F32), ALU.mult, ALU.subtract).then_inc(emptied[BANK[f"product{n}"]], 1)

                def row_max(r):
                    wait_full(dve, i, f"S2_{r}")
                    V.tensor_reduce(rowmax[:, r], ps["S"][:].rearrange("p (h k) -> p h k", h=H), AX.X, ALU.max).then_inc(rowmax_ready, 1)

                def less_max(r):
                    dve.wait_ge(rowmax_ready, NR * i + r + 1)
                    V.tensor_tensor(p2[:, r].rearrange("p (h k) -> p h k", h=H), ps["S"][:].rearrange("p (h k) -> p h k", h=H),
                                    rowmax[:, r].unsqueeze(2).broadcast_to([P, H, T]), ALU.subtract).then_inc(emptied["S"], 1)

                def row_sum(r):
                    dve.wait_ge(exp_ready, NR * i + r + 1)
                    V.tensor_reduce(rowsum[:, r], p2[:, r].rearrange("p (h k) -> p h k", h=H), AX.X, ALU.add).then_inc(rowsum_ready, 1)

                def row_inv(r):
                    dve.wait_ge(rowsum_ready, NR * i + r + 1)
                    V.reciprocal(rowinv[:, r], rowsum[:, r]).then_inc(rowinv_ready, 1)

                def allow(b):
                    wait(dve, p1_ready, NB * u + b)
                    dve.wait_ge(relu_ready, NB * u + b + 1)
                    V.scalar_tensor_tensor(allowed[:].rearrange("p (j n) -> p j n", j=J), ps[BANK[f"S1_{b}"]][:].rearrange("p (j n) -> p j n", j=J), -100.0,
                                           causal.unsqueeze(1).broadcast_to([P, J, T]), ALU.is_ge, ALU.mult).then_inc(allowed_ready, 1)

                def pieces(b):
                    dve.wait_ge(square_ready, NB * u + b + 1)
                    V.scalar_tensor_tensor(poly[:], ps[BANK[f"S1_{b}"]][:], -0.01, relu[:, b % 2], ALU.mult, ALU.max).then_inc(emptied[BANK[f"S1_{b}"]], 1)

                def p1_of(b):
                    dve.wait_ge(allowed_ready, NB * u + b + 1)
                    wait_emptied(dve, i, f"S1_{b}")
                    V.scalar_tensor_tensor(p1[:, b], poly[:], 1.0, allowed[:], ALU.add, ALU.mult).then_inc(p1_ready, 1)

                def weigh(n):
                    r, q = n // 4, n % 4
                    job = f"FF{n}"
                    wait_full(dve, i, job)
                    if f"weigh{n}" == first_of(DVE_ORDER, [f"weigh{k}" for k in range(8)]):
                        dve.wait_ge(gate_steps, GATE_STEPS * (f + 1))
                    if f"weigh{n}" == first_of(DVE_ORDER, [f"weigh{k}" for k in range(4 * r, 4 * r + 4)]):
                        if not (isinstance(i, int) and f == 0):
                            dve.wait_ge(add_steps, ADD_STEPS * f - 5 * (NR - 1 - r))
                    V.tensor_tensor(weighted[:, r, 512 * q:512 * q + 512].rearrange("p (e c) -> p e c", e=4),
                                    ps[BANK[job]][:].rearrange("p (e c) -> p e c", e=4),
                                    gate[:, r, 4 * q:4 * q + 4].unsqueeze(2).broadcast_to([P, 4, C]), ALU.mult).then_inc(emptied[BANK[job]], 1)

                def gate_of(k):
                    if k:
                        dve.wait_ge(gate_steps, GATE_STEPS * (i if k < 2 else f) + k)
                    gate_step(k).then_inc(gate_steps, 1)

                def by_row(a, n=E):
                    return a[:].unsqueeze(2).broadcast_to([P, NR, n])

                def gate_step(k):
                    if k == 0:
                        wait_emptied(dve, i, "LG")
                        return V.tensor_reduce(lmax[:], logit[:], AX.X, ALU.max)
                    if k == 1:
                        return V.tensor_tensor(logit[:], logit[:], by_row(lmax), ALU.subtract)
                    if k == 2:
                        dve.wait_ge(logit_exp_ready, f + 1)
                        return V.tensor_reduce(lsum[:], logit[:], AX.X, ALU.add)
                    if k == 3:
                        return V.reciprocal(linv[:], lsum[:])
                    if k == 4:
                        return V.tensor_tensor(prob[:, :, 0:E], logit[:], by_row(linv), ALU.mult)
                    if k in (5, 6):
                        hold_wait(k)
                        return V.max(best[:, k - 5], prob[:, k - 5, 0:E])
                    if k == 7:
                        return V.tensor_reduce(tsum[:], best[:, :, 0:TOP], AX.X, ALU.add)
                    if k == 8:
                        return V.memset(best[:, :, TOP:8], -1.0)
                    if k in (9, 10):
                        hold_wait(k)
                        return V.match_replace(left[:, k - 9], best[:, k - 9], prob[:, k - 9], 0.0)
                    if k == 11:
                        return V.tensor_scalar(tsum[:], tsum[:], TOP_EPS, None, ALU.add)
                    if k == 12:
                        return V.tensor_tensor(gate[:], prob[:, :, 0:E], left[:, :, 0:E], ALU.subtract)
                    if k == 13:
                        return V.reciprocal(tinv[:], tsum[:])
                    if k == 14:
                        return V.tensor_tensor(gate[:], gate[:], by_row(tinv), ALU.mult)
                    if k == 15:
                        return V.tensor_reduce(gsum[:], gate[:], AX.X, ALU.add)
                    if k == GEPS_STEP:
                        wait(dve, base3_ready, NR * f)
                        return V.tensor_scalar(geps[:], gsum[:], TOP_EPS, None, ALU.mult)
                    if k == 17:
                        return V.tensor_scalar(gsum[:], gsum[:], TOP_EPS, None, ALU.max)
                    if k == 18:
                        return V.reciprocal(ginv[:], gsum[:])
                    return V.tensor_tensor(gate[:], gate[:], by_row(ginv), ALU.mult)

                def move_logits():
                    wait_full(dve, i, "LG")
                    V.tensor_tensor(logit[:], ps[BANK["LG"]][:, 0:NR * E].rearrange("p (r e) -> p r e", r=NR),
                                    rb_sb[:].unsqueeze(1).broadcast_to([P, NR, E]), ALU.add).then_inc(emptied[BANK["LG"]], 1)

                def queries_lo():
                    dve.wait_ge(q_lo_ready, u + 1)
                    V.tensor_tensor(qm_lo[:], q_lo[:].rearrange("p (b t) -> p b t", b=NB).unsqueeze(2).broadcast_to([P, NB, J, T]),
                                    qmask.unsqueeze(1).unsqueeze(3).broadcast_to([P, NB, J, T]), ALU.mult).then_inc(qm_lo_ready, 1)

                def keys_lo(parity):
                    dve.wait_ge(k_hi_ready, u + 1)
                    V.scalar_tensor_tensor(kp_lo[:, :, parity], ps[BANK["K"]][:, 0:TOK].rearrange("p (b t) -> p b t", b=NB), kmask[:, parity:parity + 1],
                                           kp_hi[:, :, parity].bitcast(F32), ALU.mult, ALU.subtract).then_inc((k_lo_ready, emptied[BANK["K"]])[parity], 1)

                def projected():
                    wait_full(dve, i, "PR")
                    dve.wait_ge(x_in, 16 * (t + 1))
                    V.tensor_tensor(r1[:].rearrange("p r c -> p (r c)"), ps[BANK["PR"]][:, 0:NR * C], x_sb[:].rearrange("p r c -> p (r c)"), ALU.add).then_inc(emptied[BANK["PR"]], 1)

                def attended():
                    wait_full(dve, i, "AC1")
                    dve.wait_ge(x1b_ready, i + 1)
                    V.tensor_tensor(r2[:].rearrange("p r c -> p (r c)"), ps[BANK["AC1"]][:, 0:NR * C], x1b[:].rearrange("p r c -> p (r c)"), ALU.add).then_inc(emptied[BANK["AC1"]], 1)

                norm_stage = {1: "l1", 2: "l2", 3: "out"}
                run(i, DVE_ORDER, {"product_lo": ("setup", product_lo), "gate": (lambda k: "l2" if k < 2 else "ff", gate_of), "row_max": ("l2", row_max), "less_max": ("l2", less_max),
                                   "row_sum": ("l2", row_sum), "row_inv": ("l2", row_inv), "projected": ("l1", projected),
                                   "stats": (norm_stage.get, stats_of), "var": (norm_stage.get, var), "eps": (norm_stage.get, var_eps),
                                   "norm": (norm_stage.get, norm), "queries_lo": ("s1", queries_lo), "keys_lo": ("s1", keys_lo), "allow": ("s1", allow),
                                   "pieces": ("s1", pieces), "p1_": ("s1", p1_of), "weigh": ("ff", weigh), "attended": ("l2", attended),
                                   "logits": ("l2", move_logits)})

            turns(dve, body)

        @block.gpsimd
        def _(pool):
            G = nc.gpsimd
            pe_order = [job for job, _, _ in JOBS]
            last_context_job = last_of(pe_order, [f"VB{n}" for n in range(8)] + [f"Z{n}" for n in range(8)])
            last_expert_job = last_of(pe_order, [f"FF{n}" for n in range(8)])
            weighed = [last_of(DVE_ORDER, [f"weigh{n}" for n in range(4 * r, 4 * r + 4)]).replace("weigh", "FF") for r in range(NR)]
            G.memset(one[:], 1.0)
            G.memset(power[:], -0.5).then_inc(power_set, 1)
            pool.wait_ge(power_set, 1)

            def high(hi, src, hi_ready):
                G.tensor_tensor(hi, src, one[:].unsqueeze(1).broadcast_to([P, NB, T]), ALU.mult).then_inc(hi_ready, 1)

            def low(hi, lo, src, hi_ready, done, n):
                pool.wait_ge(hi_ready, n)
                G.tensor_tensor(lo, src, hi.bitcast(F32), ALU.subtract).then_inc(done, 1)

            def columns(a):
                return a[:].rearrange("p (b t) -> p b t", b=NB)

            pool.wait_ge(xT_in, 16)
            high(columns(xT_hi), xT[:, :, 0], xT_hi_ready)
            low(columns(xT_hi), columns(xT_lo), xT[:, :, 0], xT_hi_ready, xT_split, 1)

            def body(i):
                u, t, f = i + 2, i + 1, i - 1

                def root(n):
                    pool.wait_ge(ln_eps[n - 1], {1: t, 2: i, 3: i - 2}[n] + 1)
                    G.tensor_tensor(rstd[:, n - 1], rstd[:, n - 1], power[:], ALU.pow).then_inc(ln_rstd[n - 1], 1)

                def shares(r):
                    pool.wait_ge(rowinv_ready, NR * i + r + 1)
                    weights = p2[:, r].rearrange("p (h k) -> p h k", h=H)
                    G.tensor_tensor(weights, weights, rowinv[:, r].unsqueeze(2).broadcast_to([P, H, T]), ALU.mult).then_inc(p2_ready, 1)

                def add_experts(r, k):
                    tile = f - r
                    done = ADD_STEPS * tile + 5 * r
                    if k == 0:
                        wait_emptied(pool, i - r, weighed[r])
                    else:
                        pool.wait_ge(add_steps, done + k)
                    if k < 4:
                        width = 8 >> k
                        a, b = weighted[:, r, 0:width * C], weighted[:, r, width * C:2 * width * C]
                        G.tensor_tensor(a, a, b, ALU.add).then_inc(add_steps, 1)
                    else:
                        pool.wait_ge(base3_ready, NR * tile + r + 1)
                        if r == 0:
                            wait(pool, x3_ready, NR * tile)
                        G.tensor_tensor(r3[:, r], weighted[:, r, 0:C], base3[:, r], ALU.add).then_inc(add_steps, 1)

                def context_hi():
                    pool.wait_ge(cT_in, 16 * (t + 1))
                    if not (isinstance(i, int) and t == 0):
                        wait_full(pool, i - 1, last_context_job)
                    high(columns(cT_hi), columns(cT), cT_hi_ready)

                def context_lo():
                    low(columns(cT_hi), columns(cT_lo), columns(cT), cT_hi_ready, cT_split, t + 1)

                def next_x_hi():
                    if not isinstance(i, int) or u + 1 < NT:
                        pool.wait_ge(xT_in, 16 * (u + 2))
                        wait_full(pool, i, "V")
                        high(columns(xT_hi), xT[:, :, 0], xT_hi_ready)

                def next_x_lo():
                    if not isinstance(i, int) or u + 1 < NT:
                        low(columns(xT_hi), columns(xT_lo), xT[:, :, 0], xT_hi_ready, xT_split, u + 2)

                def queries_hi():
                    wait_emptied(pool, i, "Q")
                    G.tensor_tensor(q_hi[:].bitcast(F32R), q_sb[:], one[:].broadcast_to([P, TOK]), ALU.mult).then_inc(q_hi_ready, 1)

                def queries_lo():
                    pool.wait_ge(q_hi_ready, u + 1)
                    G.tensor_tensor(q_lo[:], q_sb[:], q_hi[:], ALU.subtract).then_inc(q_lo_ready, 1)

                def experts_hi():
                    pool.wait_ge(w_in, N_WEIGHTS)
                    pool.wait_ge(expert_in, 16)
                    G.tensor_tensor(ex_hi[:], ex_ld, one[:].broadcast_to([P, E * C]), ALU.mult).then_inc(expert_hi, 1)

                def experts_lo():
                    pool.wait_ge(expert_hi, 1)
                    G.tensor_tensor(ex_lo[:], ex_ld, ex_hi[:].bitcast(F32), ALU.subtract).then_inc(expert_split, 1)

                def x2_hi():
                    wait_emptied(pool, i, "X2T")
                    if "ff" in on(i):
                        wait_full(pool, i, last_expert_job)
                    high(columns(x2T_hi), columns(x2T), x2T_hi_ready)

                def x2_lo():
                    low(columns(x2T_hi), columns(x2T_lo), columns(x2T), x2T_hi_ready, x2T_split, i + 1)

                def bias_x1():
                    pool.wait_ge(x1_ready, NR * (t + 1))
                    if "l2" in on(i):
                        wait_emptied(pool, i, "AC1")
                    G.tensor_tensor(x1b[:], x1[:], bo_sb[:].unsqueeze(1).broadcast_to([P, NR, C]), ALU.add).then_inc(x1b_ready, 1)

                run(i, POOL_ORDER, {"experts_hi": ("setup", experts_hi), "experts_lo": ("setup", experts_lo), "context_hi": ("l1", context_hi), "context_lo": ("l1", context_lo), "next_x_hi": ("s1", next_x_hi),
                                    "next_x_lo": ("s1", next_x_lo), "q_hi": ("s1", queries_hi), "q_lo": ("s1", queries_lo), "x2_hi": ("l2", x2_hi), "x2_lo": ("l2", x2_lo),
                                    "shares": ("l2", shares), "root": ({1: "l1", 2: "l2", 3: "out"}.get, root), "bias_x1": ("l1", bias_x1),
                                    "add": (lambda r, k: ("ff", "out")[r], add_experts)})

            turns(pool, body)


def constants():
    import numpy as np
    p = np.arange(P)
    k = np.zeros((P, K_COLS), np.float32)
    k[:, K_IDENT:K_IDENT + P] = np.eye(P)
    k[:, K_CAUSAL:K_CAUSAL + T] = (p % T)[:, None] <= np.arange(T)[None, :]
    k[:, K_QMASK:K_QMASK + J] = ((p // (2 * HD))[:, None] == np.arange(J)[None, :])
    k[:, K_KMASK:K_KMASK + 2] = (p // HD % 2)[:, None] == np.arange(2)[None, :]
    return k


def kernel(x, ctx_1024, L0_attn_W_attn, L0_attn_W_proj, L0_xattn_WQ, L0_xattn_WK, L0_xattn_WV, L0_xattn_WO,
           L0_xattn_bO, L0_ffn_router_w, L0_ffn_router_b, L0_ffn_expert_w):
    import numpy as np
    import concourse.bacc as bacc
    from concourse.bass_utils import run_bass_kernel_spmd

    def columns(a):
        return np.asarray(a).reshape(NT, TOK, C).transpose(0, 2, 1)

    def by_pair(w):
        return np.asarray(w).T.reshape(J, P, C).transpose(1, 0, 2).reshape(P, J * C)

    twice = np.repeat(columns(x).reshape(NT, C, NB, 1, T), 2, axis=3)
    arrays = {
        "x": x, "x_t": twice, "ctx_t": columns(ctx_1024), "w_attn": L0_attn_W_attn, "w_proj": L0_attn_W_proj,
        "wq_t": by_pair(L0_xattn_WQ), "wk_t": by_pair(L0_xattn_WK), "wv_t": by_pair(L0_xattn_WV), "wo": L0_xattn_WO,
        "b_o": L0_xattn_bO, "router_t": np.asarray(L0_ffn_router_w).T, "router_b": L0_ffn_router_b,
        "expert_w": L0_ffn_expert_w, "consts": constants(),
    }
    arrays = {n: np.ascontiguousarray(a) for n, a in arrays.items()}
    nc = bacc.Bacc("TRN2", target_bir_lowering=False, num_devices=1)
    args = {n: nc.dram_tensor("in_" + n, a.shape, mybir.dt.from_np(a.dtype), kind="ExternalInput").ap() for n, a in arrays.items()}
    out = nc.dram_tensor("out_0", (B, T, C), F32, kind="ExternalOutput").ap()
    decoder(nc, out=out, **args)
    r = run_bass_kernel_spmd(nc, [{"in_" + n: a for n, a in arrays.items()}], core_ids=[0])
    return r.results[0]["out_0"]
```
